# Optimizing a Trainium2 kernel written in Bass

```python
import numpy as np
import jax
import jax.numpy as jnp

def _softmax(x, axis=-1):
    return jax.nn.softmax(x, axis=axis)

def _gelu(x):
    return jax.nn.gelu(x, approximate=True)

def _silu(x):
    return jax.nn.silu(x)

def _sigmoid(x):
    return jax.nn.sigmoid(x)

def _layernorm(x, axis=-1, eps=1e-05):
    m = jnp.mean(x, axis=axis, keepdims=True)
    v = jnp.var(x, axis=axis, keepdims=True)
    return (x - m) / jnp.sqrt(v + eps)

def _scatter_add(tgt, idx, src, axis=0):
    return tgt.at[idx].add(src)

def _segment_sum(src, seg, n):
    return jax.ops.segment_sum(src, seg, n)
kernel_name = 'mk_adj_preln_d2_adj_r2_517814'

def setup_inputs(seed: int=0):
    np.random.seed(seed)
    _w = jnp.asarray

    def _rec_inputs():
        import jax
        import jax.numpy as jnp
        _gk = jax.random.key(seed)
        x = 0.0001732 + 1 * jax.random.normal(jax.random.fold_in(_gk, 1), (5120, 64), jnp.float32)
        _a = jax.random.bernoulli(jax.random.fold_in(_gk, 2), 0.0015625, (5120, 5120))
        _af = _a.astype(jnp.float32)
        _af = _af * jax.random.uniform(jax.random.fold_in(_gk, 3), (5120, 5120), jnp.float32, 0.05, 0.02)
        adj = _af
        return (x, adj)
    x, adj = _rec_inputs()

    def _L0_gnn_setup():
        import jax, jax.numpy as jnp
        import numpy as np
        N_USERS = 2048
        N_ITEMS = 3072
        EMB = 64
        LN_EPS = 1e-05
        key = jax.random.key(seed)
        ks = jax.random.split(key, 10)
        N = N_USERS + N_ITEMS
        ego = jax.random.normal(ks[0], (N, EMB), jnp.float32)
        adj = (jax.random.uniform(ks[1], (N, N), jnp.float32) < 0.01).astype(jnp.float32) * 0.02
        xav = float(np.sqrt(6.0 / (EMB + EMB)))
        W_u = jax.random.uniform(ks[2], (EMB, EMB), jnp.float32, -xav, xav)
        W_i = jax.random.uniform(ks[3], (EMB, EMB), jnp.float32, -xav, xav)
        diag_u = jax.random.uniform(ks[4], (N_USERS,), jnp.float32, 0.99, 1.01)
        diag_i = jax.random.uniform(ks[5], (N_ITEMS,), jnp.float32, 0.99, 1.01)
        par_u = jax.random.uniform(ks[6], (2,), jnp.float32, 0.0, 0.99)
        par_i = jax.random.uniform(ks[7], (2,), jnp.float32, 0.0, 0.99)
        ln_gamma = jnp.ones((EMB,), jnp.float32)
        ln_beta = jnp.zeros((EMB,), jnp.float32)
        return {'ego_embeddings': ego, 'adj': adj, 'W_u': W_u, 'diag_u': diag_u, 'par_u': par_u, 'W_i': W_i, 'diag_i': diag_i, 'par_i': par_i, 'ln_gamma': ln_gamma, 'ln_beta': ln_beta}
    _L0_gnn_all = _L0_gnn_setup()
    _L0_gnn_in = {k: v for k, v in _L0_gnn_all.items() if k in ('W_u', 'diag_u', 'par_u', 'W_i', 'diag_i', 'par_i', 'ln_gamma', 'ln_beta')}
    del _L0_gnn_all

    def _L1_gnn_setup():
        import jax, jax.numpy as jnp
        import numpy as np
        N = 8192
        F = 64
        O = 64
        key = jax.random.key(seed)
        k1, k2, k3 = jax.random.split(key, 3)
        features = jax.random.normal(k1, (N, F), dtype=jnp.float32)
        adj = jax.random.uniform(k2, (N, N), dtype=jnp.float32)
        W = jax.random.normal(k3, (O, 2 * F), dtype=jnp.float32)
        return {'features': features, 'adj': adj, 'W': W}
    _L1_gnn_all = _L1_gnn_setup()
    _L1_gnn_in = {k: v for k, v in _L1_gnn_all.items() if k in ('W',)}
    del _L1_gnn_all
    return {'x': x, 'adj': adj, 'L0_gnn_W_u': _L0_gnn_in['W_u'], 'L0_gnn_diag_u': _L0_gnn_in['diag_u'], 'L0_gnn_par_u': _L0_gnn_in['par_u'], 'L0_gnn_W_i': _L0_gnn_in['W_i'], 'L0_gnn_diag_i': _L0_gnn_in['diag_i'], 'L0_gnn_par_i': _L0_gnn_in['par_i'], 'L0_gnn_ln_gamma': _L0_gnn_in['ln_gamma'], 'L0_gnn_ln_beta': _L0_gnn_in['ln_beta'], 'L1_gnn_W': _L1_gnn_in['W']}

def reference(x, adj, L0_gnn_W_u, L0_gnn_diag_u, L0_gnn_par_u, L0_gnn_W_i, L0_gnn_diag_i, L0_gnn_par_i, L0_gnn_ln_gamma, L0_gnn_ln_beta, L1_gnn_W):
    import jax
    import jax.numpy as jnp

    def _L0_gnn_ref(ego_embeddings, adj, W_u, diag_u, par_u, W_i, diag_i, par_i, ln_gamma, ln_beta):
        import jax, jax.numpy as jnp
        import numpy as np
        N_USERS = 2048
        N_ITEMS = 3072
        EMB = 64
        LN_EPS = 1e-05
        nu = diag_u.shape[0]
        res = ego_embeddings
        ego_u = ego_embeddings[:nu]
        ego_i = ego_embeddings[nu:]
        u = par_u[0] * par_u[1] * (diag_u[:, None] * ego_u @ W_u) + ego_u
        i = par_i[0] * par_i[1] * (diag_i[:, None] * ego_i @ W_i) + ego_i
        e = jnp.concatenate([u, i], axis=0)
        h = adj @ (adj.T @ e)
        mu = jnp.mean(h, axis=-1, keepdims=True)
        var = jnp.var(h, axis=-1, keepdims=True)
        out = (h - mu) * jax.lax.rsqrt(var + LN_EPS) * ln_gamma + ln_beta + res
        return out

    def _L1_gnn_ref(features, adj, W):
        import jax, jax.numpy as jnp
        import numpy as np
        N = 8192
        F = 64
        O = 64
        deg = jnp.sum(adj, axis=1, keepdims=True)
        neigh = adj @ features / (deg + 1.0)
        data = jnp.concatenate([features, neigh], axis=-1)
        return data @ W.T
    h = jnp.maximum(_layernorm(x, axis=-1), 0.0)
    x = x + _L0_gnn_ref(h, adj, L0_gnn_W_u, L0_gnn_diag_u, L0_gnn_par_u, L0_gnn_W_i, L0_gnn_diag_i, L0_gnn_par_i, L0_gnn_ln_gamma, L0_gnn_ln_beta)
    h = jnp.maximum(_layernorm(x, axis=-1), 0.0)
    x = x + _L1_gnn_ref(h, adj, L1_gnn_W)
    return x

_drawn_inputs = setup_inputs


def setup_inputs(seed=0):
    import zlib

    import numpy as np

    out = dict(_drawn_inputs(seed))
    spreads = {'L0_gnn_ln_gamma': (1.0, 0.2), 'L0_gnn_ln_beta': (0.0, 0.1)}
    factors = {}
    for name, (base, spread) in spreads.items():
        noise = np.random.default_rng([zlib.crc32(name.encode()), seed]).standard_normal(out[name].shape)
        drawn = base * np.exp(spread * noise) if base else spread * noise
        out[name] = jnp.asarray(drawn.astype(out[name].dtype))
    for name, factor in factors.items():
        out[name] = (out[name] * factor).astype(out[name].dtype)
    return out
```

```python
from contextlib import ExitStack

import concourse.bass as bass
from concourse import mybir

F32 = mybir.dt.float32
BF16 = mybir.dt.bfloat16
ALU = mybir.AluOpType
ACT = mybir.ActivationFunctionType
AX = mybir.AxisListType

P = 128
N = 5120
D = 64
EPS = 1e-5
NT = N // P
W = 512
CB = W // P
NBLK = N // W
KR = CB
KN = NT - KR
QS = (N - W) // 4
LAST = N - W
BANK = 512
G = BANK // D
NG = NT // G
AG = 2
ASLOTS = 5
BG = 2
BSLOTS = 4
BT = 4
OG = 8
SMALL = 16
EARLY = 8
N_USERS = 2048
KU = (N_USERS - QS) // 32
ORDER = [NG - 1] + list(range(NG - 1))
assert NT % (AG * ASLOTS) == 0 and KN % BT == 0 and 4 * BT % (BG * BSLOTS) == 0 and KN * 32 == QS


def early_after(k):
    return (k - 8) // 4 if k >= 8 and k % 4 == 0 else None


def build(nc, x, adj, W_u, diag_u, par_u, W_i, diag_i, par_i, gamma, beta, W1, out):
    with ExitStack() as ctx:
        def sb(name, shape, dt=F32):
            return ctx.enter_context(nc.sbuf_tensor(name, shape, dt))

        def sem(name):
            return ctx.enter_context(nc.semaphore(name))

        kept = sb("kept", [P, NT, CB, P])
        xr = sb("xr", [P, NT, D])
        eg = sb("eg", [P, NT, D])
        anat = sb("anat", [P, ASLOTS * AG, W])
        bnat = sb("bnat", [P, BSLOTS * BG, QS])
        bT = sb("bT", [P, 2, KN, P])
        tsb = sb("tsb", [P, CB, D])
        ident = sb("ident", [P, P])
        zeros = sb("zeros", [P, BANK], BF16)
        degp = sb("degp", [P, NT, NBLK])
        deg = sb("deg", [P, NT])
        deg1 = sb("deg1", [P, NT])
        rdeg = sb("rdeg", [P, NT])
        dtab = sb("dtab", [NT, 2, P])
        coef = sb("coef", [P, 2, NT])
        par = sb("par", [P, 2, 2])
        parp = sb("parp", [P, 2])
        wui = sb("wui", [P, D])
        wst = sb("wst", [P, 4, P])
        wbd = sb("wbd", [P, 4, D])
        gam = sb("gam", [P, D])
        bet = sb("bet", [P, D])
        eps = sb("eps", [P, 1])
        fT = sb("fT", [P, G // 2, P])
        st = sb("st", [P, 4, G, 6])
        mv = sb("mv", [P, 4, G, 2])
        sd = sb("sd", [P, 4, G])
        rs = sb("rs", [P, 4, G])
        nm = sb("nm", [P, 2, G])
        h0 = bT[:, 0, 0:NT // 2, :].rearrange("p a (b d) -> p (a b) d", b=2)
        h2 = bT[:, 1, 0:G, :].rearrange("p g (s d) -> p g s d", s=2)
        hT = bT[:, 1, G:2 * G, :]

        ps = ctx.enter_context(nc.psum_tensor("ps", [P, 8 * BANK], F32))
        TBANK, TR = NG, NG + 1

        def bank(b, n=BANK):
            return ps[:, b * BANK:b * BANK + n]

        hacc = ps[:, 0:NG * BANK].rearrange("p (k d) -> p k d", d=D)
        tacc = bank(TBANK, CB * D).rearrange("p (c d) -> p c d", d=D)

        def nacc(k):
            at = (k % NG) * BANK + (k // NG) * D
            return ps[:, at:at + D] if isinstance(k, int) else ps[:, bass.ds(at, D)]

        x_landed = sem("x_landed")
        small_landed = sem("small_landed")
        a_landed = [sem(f"a_landed{s}") for s in range(ASLOTS)]
        b_landed = [sem(f"b_landed{s}") for s in range(BSLOTS)]
        out_stored = sem("out_stored")
        zeroed = sem("zeroed")
        consts = sem("consts")
        tabs_T = sem("tabs_T")
        tabs = sem("tabs")
        vec = sem("vec")
        pool_own = sem("pool_own")
        h0_var = sem("h0_var")
        h0_sd = sem("h0_sd")
        h0_rs = sem("h0_rs")
        h0_ready = sem("h0_ready")
        h2_ready = sem("h2_ready")
        h2_T = sem("h2_T")
        hT_ready = sem("hT_ready")
        hw_done = sem("hw_done")
        e_ready = sem("e_ready")
        deg_summed = sem("deg_summed")
        t_done = sem("t_done")
        t_ready = sem("t_ready")
        a2_done = sem("a2_done")
        tile_T = sem("tile_T")
        tile_kept = sem("tile_kept")
        h_done = sem("h_done")
        h_copied = sem("h_copied")
        hn_var = sem("hn_var")
        hn_sd = sem("hn_sd")
        hn_ready = sem("hn_ready")
        x2_ready = sem("x2_ready")
        x2_var = sem("x2_var")
        x2_sd = sem("x2_sd")
        x2_rs = sem("x2_rs")
        f_ready = sem("f_ready")
        f_T = sem("f_T")
        fT_ready = sem("fT_ready")
        y_done = sem("y_done")
        y_added = sem("y_added")
        g_ready = sem("g_ready")
        unit_T = sem("unit_T")
        row_done = sem("row_done")
        row_final = sem("row_final")
        xrb_ready = sem("xrb_ready")

        block = ctx.enter_context(nc.Block())


        def a_landed_count(i, k):
            return (i * (NT // (AG * ASLOTS)) + k // (AG * ASLOTS) + 1) * 64

        @block.sync
        def _(sp):
            for q in range(4):
                sp.dma_start(xr[32 * q:32 * q + 32, 0:KN, :],
                             x[q * QS:(q + 1) * QS, :].rearrange("(k r) d -> r k d", r=32)).then_inc(x_landed, 16)
            sp.dma_start(xr[:, KN:NT, :], x[LAST:N, :].rearrange("(k p) d -> p k d", p=P)).then_inc(x_landed, 16)

            def load_a(i, k, c0):
                n = i * NT + k
                s, y = k // AG % ASLOTS, k % (AG * ASLOTS)
                if not (isinstance(i, int) and n < AG * ASLOTS):
                    freed = n - AG * ASLOTS + AG
                    sp.wait_ge(tile_T, freed)
                    sp.wait_ge(deg_summed, freed)
                for q in (0, 2, 1, 3):
                    if k < KN:
                        src = adj[q * QS + 32 * k:q * QS + 32 * (k + AG), c0].rearrange("(y r) c -> r y c", r=32)
                    else:
                        src = adj[LAST + (k - KN) * P:LAST + (k - KN + AG) * P, c0].rearrange(
                            "(y q r) c -> q r y c", q=4, r=32)[q]
                    sp.dma_start(anat[32 * q:32 * q + 32, y:y + AG, :], src).then_inc(a_landed[s], 16)

            def load_b(i, u, last=False):
                j, R = u // 4, u % 4
                s, y = u // BG % BSLOTS, u % (BG * BSLOTS)
                for q in (0, 2, 1, 3):
                    cols = slice(q * QS, (q + 1) * QS)
                    if last:
                        r0 = LAST + j * P + 32 * R
                        src = adj[r0:r0 + BG * 32, cols].rearrange("(R r) c -> r R c", r=32)
                    else:
                        src = adj[0:LAST, cols].rearrange("(R k r) c -> k r R c", R=4, r=32)[
                            bass.ds(i * BT + j, 1), :, R:R + BG, :].rearrange("k r R c -> (k r) R c")
                    sp.dma_start(bnat[32 * q:32 * q + 32, y:y + BG, :], src).then_inc(b_landed[s], 16)

            for k in range(0, NT, AG):
                load_a(0, k, slice(0, W))
            with sp.Fori(1, NBLK - 1) as i:
                for k in range(0, NT, AG):
                    load_a(i, k, bass.ds(i * W, W))
            for k in range(0, NT, AG):
                load_a(NBLK - 1, k, slice(LAST, N))
                u = early_after(k)
                if u is not None and u % BG == 0:
                    load_b(0, u)
            for u in range(EARLY, 4 * BT, BG):
                sp.wait_ge(unit_T, u - BSLOTS * BG + BG)
                load_b(0, u)
            with sp.Fori(1, KN // BT) as i:
                for u in range(0, 4 * BT, BG):
                    sp.wait_ge(unit_T, i * (4 * BT) + (u - BSLOTS * BG + BG))
                    load_b(i, u)
            for u in range(0, 4 * BT, BG):
                sp.wait_ge(unit_T, KN * 4 + u - BSLOTS * BG + BG)
                load_b(KN // BT, u, last=True)

        @block.gpsimd
        def _(pool):
            nc.gpsimd.memset(ident[:], 0.0).then_inc(pool_own, 1)
            nc.gpsimd.memset(zeros[:], 0.0).then_inc(consts, 1)
            nc.gpsimd.memset(eps[:], EPS).then_inc(consts, 1)
            pool.wait_ge(pool_own, 1)
            nc.gpsimd.affine_select(out=ident[:], in_=ident[:], compare_op=ALU.not_equal, fill=1.0, base=0,
                                    pattern=[[-1, P]], channel_multiplier=1).then_inc(consts, 1)
            own = 1
            pool.wait_ge(tabs, 2)
            pool.wait_ge(small_landed, 16 * SMALL)
            for g in range(NG):
                ks = slice(g * G, g * G + G)
                pool.wait_ge(h0_ready, g + 1)
                if g >= 1:
                    pool.wait_ge(h2_T, g)
                for s in range(2):
                    nc.gpsimd.tensor_tensor(h2[:, :, s, :], h0[:, ks, :],
                                            coef[:, s, ks].unsqueeze(2).to_broadcast([P, G, D]),
                                            ALU.mult).then_inc(h2_ready, 1)
            for g in range(NG):
                ks = slice(g * G, g * G + G)
                nc.gpsimd.tensor_tensor(xr[:, ks, :], xr[:, ks, :], h0[:, ks, :], ALU.add).then_inc(pool_own, 1)
                own += 1
                pool.wait_ge(pool_own, own)
                nc.gpsimd.tensor_tensor(xr[:, ks, :], xr[:, ks, :], bet[:].unsqueeze(1).to_broadcast([P, G, D]),
                                        ALU.add).then_inc(xrb_ready, 1)
            pool.wait_ge(xrb_ready, NG)
            for c, g in enumerate(ORDER):
                ks = slice(g * G, g * G + G)
                pool.wait_ge(hn_ready, c + 1)
                nc.gpsimd.tensor_tensor(eg[:, ks, :], eg[:, ks, :], gam[:].unsqueeze(1).to_broadcast([P, G, D]),
                                        ALU.mult).then_inc(pool_own, 1)
                own += 1
                pool.wait_ge(pool_own, own)
                nc.gpsimd.tensor_tensor(xr[:, ks, :], xr[:, ks, :], eg[:, ks, :], ALU.add).then_inc(x2_ready, 1)

        @block.tensor
        def _(pe):
            pe.wait_ge(consts, 3)
            pe.wait_ge(small_landed, 16 * SMALL)
            for s in range(2):
                nc.tensor.transpose(bank(0)[:, s * NT:(s + 1) * NT], dtab[:, s, :], ident[0:NT, 0:NT])
            for s in range(4):
                mm = nc.tensor.transpose(bank(1)[:, s * P:(s + 1) * P], wst[:, s, :], ident[:])
            mm.then_inc(tabs_T, 1)

            def e_group(g):
                pe.wait_ge(h2_ready, 2 * g + 2)
                if g == 0:
                    pe.wait_ge(tabs, 2)
                if g >= 1:
                    pe.wait_ge(hT_ready, 2 * g)
                for y in range(G):
                    mm = nc.tensor.transpose(ps[:, y * P:(y + 1) * P], h2[:, y, :, :], ident[:])
                mm.then_inc(h2_T, 1)
                pe.wait_ge(hT_ready, 2 * g + 2)
                if g >= 1:
                    pe.wait_ge(e_ready, g)
                for y in range(G):
                    mm = nc.tensor.matmul(bank(2)[:, y * D:(y + 1) * D], hT[:, y, :], wui[:], start=True, stop=True)
                mm.then_inc(hw_done, 1)

            def product_t(i, k):
                n = i * NT + k
                pe.wait_ge(a_landed[k // AG % ASLOTS], a_landed_count(i, k))
                if k == 0 and not (isinstance(i, int) and i == 0):
                    pe.wait_ge(t_ready, i)
                for c in range(CB):
                    mm = nc.tensor.matmul(tacc[:, c, :], anat[:, k % (AG * ASLOTS), c * P:(c + 1) * P], eg[:, k, :],
                                          start=(k == 0 and c == 0), stop=(k == NT - 1), skip_group_check=True)
                if k == NT - 1:
                    mm.then_inc(t_done, 1)

            def product_h(i, k):
                pe.wait_ge(tile_kept, i * NT + k + 1)
                if k == 0:
                    pe.wait_ge(t_ready, i + 1)
                for c in range(CB):
                    mm = nc.tensor.matmul(hacc[:, k, :], kept[:, k, c, :], tsb[:, c, :],
                                          start=False, stop=False, skip_group_check=True)
                return mm

            def transposes(i, k):
                n = i * NT + k
                if not (isinstance(i, int) and n < 2):
                    pe.wait_ge(tile_kept, n - 1)
                for c in range(CB):
                    mm = nc.tensor.transpose(bank(TR + k % 2)[:, c * P:(c + 1) * P],
                                             anat[:, k % (AG * ASLOTS), c * P:(c + 1) * P], ident[:])
                mm.then_inc(tile_T, 1)

            def block_steps(i):
                for k in range(NT - 2):
                    product_t(i, k)
                    product_h(i - 1, k)
                    transposes(i, k)
                product_t(i, NT - 2)
                product_t(i, NT - 1)
                product_h(i - 1, NT - 2)
                product_h(i - 1, NT - 1).then_inc(a2_done, 1)
                transposes(i, NT - 2)
                transposes(i, NT - 1)

            e_group(0)
            for k in range(NT):
                if k % G == 0:
                    pe.wait_ge(e_ready, k // G + 1)
                product_t(0, k)
                transposes(0, k)
                if k % G == 3 and k // G + 1 < NG:
                    e_group(k // G + 1)
            for b in range(NG):
                nc.tensor.matmul(bank(b), zeros[:, 0:P], zeros[:], start=True, stop=False, skip_group_check=True)
            with pe.Fori(1, NBLK - 1) as i:
                block_steps(i)
            block_steps(NBLK - 1)
            pe.wait_ge(t_ready, NBLK)
            for g in ORDER:
                for k in range(g * G, g * G + G):
                    mm = product_h(NBLK - 1, k)
                mm.then_inc(h_done, 1)

            def g_group(c):
                g = ORDER[c]
                pe.wait_ge(f_ready, c + 1)
                if c >= 1:
                    pe.wait_ge(fT_ready, c)
                for y in range(0, G, 2):
                    mm = nc.tensor.transpose(bank(TR)[:, y * D:y * D + P], eg[:, g * G + y:g * G + y + 2, :], ident[:])
                mm.then_inc(f_T, 1)

            def gw_group(c):
                pe.wait_ge(fT_ready, c + 1)
                if c >= 1:
                    pe.wait_ge(y_added, c)
                    pe.wait_ge(g_ready, c)
                for y in range(G):
                    nc.tensor.matmul(bank(TR + 1)[:, y * D:(y + 1) * D], fT[:, y // 2, :], wbd[:, y % 2, :],
                                     start=True, stop=True)
                for y in range(G):
                    mm = nc.tensor.matmul(bank(TBANK)[:, y * D:(y + 1) * D], fT[:, y // 2, :], wbd[:, 2 + y % 2, :],
                                          start=True, stop=True)
                mm.then_inc(y_done, 1)

            def kept_share(k):
                for c in range(CB):
                    nc.tensor.matmul(nacc(k), kept[:, k, c, :], eg[:, KN + c, :],
                                     start=(k < NG and c == 0), stop=False, skip_group_check=True)

            for c in range(NG):
                g_group(c)
                gw_group(c)
                if c >= 1:
                    pe.wait_ge(h_copied, NG)
                    pe.wait_ge(g_ready, 1)
                    for k in range((c - 1) * 10, c * 10):
                        kept_share(k)
            pe.wait_ge(g_ready, NG)

            with pe.Fori(0, NT // BT) as i:
                for j in range(BT):
                    k = i * BT + j
                    pe.wait_ge(unit_T, k * 4 + 4)
                    for kk in range(KN):
                        mm = nc.tensor.matmul(nacc(k), bT[:, j % 2, kk, :], eg[:, kk, :],
                                              start=False, stop=(kk == KN - 1), skip_group_check=True)
                    mm.then_inc(row_done, 1)

        @block.scalar
        def _(act):
            def small(dst, src):
                act.dma_start(dst, src).then_inc(small_landed, 16)

            act.wait_ge(zeroed, 2)
            small(dtab[0:KN, 0, 0:32], diag_u[0:QS].rearrange("(k r) -> k r", r=32))
            small(dtab[0:KU, 0, 32:64], diag_u[QS:N_USERS].rearrange("(k r) -> k r", r=32))
            small(dtab[KU:KN, 1, 32:64], diag_i[0:2 * QS - N_USERS].rearrange("(k r) -> k r", r=32))
            for q in (2, 3):
                small(dtab[0:KN, 1, 32 * q:32 * q + 32],
                      diag_i[q * QS - N_USERS:(q + 1) * QS - N_USERS].rearrange("(k r) -> k r", r=32))
            small(dtab[KN:NT, 1, :], diag_i[LAST - N_USERS:].rearrange("(k p) -> k p", p=P))
            small(par[:, 0, :], par_u.partition_broadcast(P))
            small(par[:, 1, :], par_i.partition_broadcast(P))
            small(wui[0:D, :], W_u)
            small(wui[D:P, :], W_i)
            for s in range(2):
                small(wst[0:D, 2 * s, 0:D], W1[:, s * D:(s + 1) * D])
                small(wst[0:D, 2 * s + 1, D:P], W1[:, s * D:(s + 1) * D])
            small(gam[:], gamma.partition_broadcast(P))
            small(bet[:], beta.partition_broadcast(P))

            def h0_std(g):
                act.wait_ge(h0_var, g + 1)
                nc.scalar.activation(sd[:, g % 2, :], mv[:, g % 2, :, 1], ACT.Sqrt, bias=eps[:]).then_inc(h0_sd, 1)

            def h0_relu(g):
                act.wait_ge(h0_rs, g + 1)
                for y in range(G):
                    a = nc.scalar.activation(h0[:, g * G + y, :], xr[:, g * G + y, :], ACT.Relu,
                                             bias=nm[:, g % 2, y:y + 1], scale=rs[:, g % 2, y:y + 1])
                a.then_inc(h0_ready, 1)

            def hT_copy(g):
                act.wait_ge(h2_T, g + 1)
                if g >= 1:
                    act.wait_ge(hw_done, g)
                for s in range(2):
                    nc.scalar.copy(hT[:, s * (G // 2):(s + 1) * (G // 2), :],
                                   bank(s).rearrange("p (y r) -> p y r", r=P)).then_inc(hT_ready, 1)

            def keep(i, k):
                act.wait_ge(tile_T, i * NT + k + 1)
                nc.scalar.copy(kept[:, k, :, :], bank(TR + k % 2).rearrange("p (c r) -> p c r", r=P)
                               ).then_inc(tile_kept, 1)

            def copy_t(i, first=False):
                act.wait_ge(t_done, i + 1)
                if not first:
                    act.wait_ge(a2_done, i)
                nc.scalar.copy(tsb[:], tacc).then_inc(t_ready, 1)

            act.wait_ge(consts, 3)
            h0_std(0)
            h0_relu(0)
            h0_std(1)
            hT_copy(0)
            h0_relu(1)
            for k in range(NT):
                keep(0, k)
                if k % G == 3:
                    g = k // G + 1
                    if g < NG:
                        hT_copy(g)
                    if g + 1 < NG:
                        h0_std(g + 1)
                        h0_relu(g + 1)
            copy_t(0, first=True)
            with act.Fori(1, NBLK - 1) as i:
                for k in range(NT - 2):
                    keep(i, k)
                copy_t(i)
                keep(i, NT - 2)
                keep(i, NT - 1)
            for k in range(NT - 2):
                keep(NBLK - 1, k)
            copy_t(NBLK - 1)
            keep(NBLK - 1, NT - 2)
            keep(NBLK - 1, NT - 1)

            for c, g in enumerate(ORDER):
                act.wait_ge(h_done, c + 1)
                nc.scalar.copy(eg[:, g * G:(g + 1) * G, :], hacc[:, g * G:(g + 1) * G, :]).then_inc(h_copied, 1)

            def std(c, which, have, give):
                act.wait_ge(have, c + 1)
                nc.scalar.activation(sd[:, which, :], mv[:, which, :, 1], ACT.Sqrt, bias=eps[:]).then_inc(give, 1)

            for s in range(NG + 4):
                if s < NG:
                    std(s, s % 2, hn_var, hn_sd)
                c = s - 2
                if 0 <= c < NG:
                    std(c, 2 + c % 2, x2_var, x2_sd)
                    act.wait_ge(x2_rs, c + 1)
                    g = ORDER[c]
                    for y in range(G):
                        a = nc.scalar.activation(eg[:, g * G + y, :], xr[:, g * G + y, :], ACT.Relu,
                                                 bias=nm[:, c % 2, y:y + 1], scale=rs[:, 2 + c % 2, y:y + 1])
                    a.then_inc(f_ready, 1)
                c = s - 2
                if 0 <= c < NG:
                    act.wait_ge(f_T, c + 1)
                    if c >= 1:
                        act.wait_ge(y_done, c)
                    nc.scalar.copy(fT[:], bank(TR).rearrange("p (y r) -> p y r", r=P)).then_inc(fT_ready, 1)
                c = s - 3
                if 0 <= c < NG:
                    g = ORDER[c]
                    act.wait_ge(y_done, c + 1)
                    nc.scalar.copy(eg[:, g * G:(g + 1) * G, :],
                                   bank(TBANK).rearrange("p (y d) -> p y d", d=D)).then_inc(g_ready, 1)

            for k in range(0, KN, OG):
                m = min(OG, KN - k)
                act.wait_ge(row_final, k + m)
                for q in range(4):
                    act.dma_start(out[q * QS + 32 * k:q * QS + 32 * (k + m), :].rearrange("(y r) d -> r y d", r=32),
                                  xr[32 * q:32 * q + 32, k:k + m, :]).then_inc(out_stored, 16)
            act.wait_ge(row_final, NT)
            act.dma_start(out[LAST:N, :].rearrange("(k p) d -> p k d", p=P), xr[:, KN:NT, :]).then_inc(out_stored, 16)
            act.wait_ge(out_stored, 16 * (4 * ((KN + OG - 1) // OG) + 1))

        @block.vector
        def _(dve):
            own = [0]

            def link(ins):
                own[0] += 1
                ins.then_inc(vec, 1)
                dve.wait_ge(vec, own[0])

            nc.vector.memset(dtab[:], 0.0).then_inc(zeroed, 1)
            nc.vector.memset(wst[:], 0.0).then_inc(zeroed, 1)
            dve.wait_ge(small_landed, 16 * SMALL)
            link(nc.vector.tensor_tensor(parp[:], par[:, :, 0], par[:, :, 1], ALU.mult))
            dve.wait_ge(tabs_T, 1)
            nc.vector.tensor_copy(wbd[:], bank(1).rearrange("p (s c) -> p s c", c=P)[:, :, 0:D]).then_inc(tabs, 1)
            nc.vector.tensor_tensor(coef[:], bank(0, 2 * NT).rearrange("p (s k) -> p s k", s=2),
                                    parp[:].unsqueeze(2).to_broadcast([P, 2, NT]), ALU.mult).then_inc(tabs, 1)

            def moments(src, which, give):
                for y in range(G):
                    ins = nc.vector.bn_stats(st[:, which, y, :], src[:, y, :])
                link(ins)
                for y in range(G):
                    ins = nc.vector.bn_aggr(mv[:, which, y, :], st[:, which, y, :])
                ins.then_inc(give, 1)

            def reciprocal(which, have, c):
                dve.wait_ge(have, c + 1)
                link(nc.vector.reciprocal(rs[:, which, :], sd[:, which, :]))

            def neg_mean(slot, which, give):
                nc.vector.scalar_tensor_tensor(out=nm[:, slot, :], in0=mv[:, which, :, 0], scalar=-1.0,
                                               in1=rs[:, which, :], op0=ALU.mult, op1=ALU.mult).then_inc(give, 1)

            def h0_moments(g):
                moments(xr[:, g * G:(g + 1) * G, :], g % 2, h0_var)

            def h0_scale(g):
                reciprocal(g % 2, h0_sd, g)
                if g >= 2:
                    dve.wait_ge(h0_ready, g - 1)
                neg_mean(g % 2, g % 2, h0_rs)

            def make_e(g):
                dve.wait_ge(hw_done, g + 1)
                dve.wait_ge(h0_ready, g + 1)
                nc.vector.tensor_tensor(eg[:, g * G:(g + 1) * G, :], bank(2).rearrange("p (y d) -> p y d", d=D),
                                        h0[:, g * G:(g + 1) * G, :], ALU.add).then_inc(e_ready, 1)

            def row_sum(i, k):
                dve.wait_ge(a_landed[k // AG % ASLOTS], a_landed_count(i, k))
                nc.vector.tensor_reduce(degp[:, k, bass.ds(i, 1)], anat[:, k % (AG * ASLOTS), :], AX.X, ALU.add
                                        ).then_inc(deg_summed, 1)

            dve.wait_ge(x_landed, 16 * 5)
            h0_moments(0)
            h0_moments(1)
            h0_scale(0)
            h0_scale(1)
            make_e(0)
            for k in range(NT):
                row_sum(0, k)
                g = k // G + 1
                if k % G == 0 and g + 1 < NG:
                    dve.wait_ge(h0_ready, g)
                    h0_moments(g + 1)
                if k % G == 1 and g + 1 < NG:
                    h0_scale(g + 1)
                if k % G == 3 and g < NG:
                    make_e(g)
            with dve.Fori(1, NBLK - 1) as i:
                for k in range(NT):
                    row_sum(i, k)

            def unit(k, R, j):
                u = 4 * j + R
                loads = (k - j) * 4 // (BG * BSLOTS) + u // (BG * BSLOTS) + 1
                dve.wait_ge(b_landed[u // BG % BSLOTS], loads * 64)
                nc.vector.transpose(bT[:, j % 2, :, 32 * R:32 * R + 32], bnat[:, u % (BG * BSLOTS), :]
                                    ).then_inc(unit_T, 1)

            for k in range(NT):
                row_sum(NBLK - 1, k)
                if early_after(k) is not None:
                    u = early_after(k)
                    if u == 0:
                        dve.wait_ge(xrb_ready, NG)
                    unit(u // 4, u % 4, u // 4)

            dve.wait_ge(deg_summed, NBLK * NT)
            link(nc.vector.tensor_reduce(deg[:], degp[:], AX.X, ALU.add))
            link(nc.vector.tensor_scalar(deg1[:], deg[:], 1.0, None, ALU.add))
            link(nc.vector.reciprocal(rdeg[:], deg1[:]))

            for s in range(NG + 4):
                if s < NG:
                    g = ORDER[s]
                    dve.wait_ge(h_copied, s + 1)
                    moments(eg[:, g * G:(g + 1) * G, :], s % 2, hn_var)
                c = s - 2
                if 0 <= c < NG:
                    g = ORDER[c]
                    dve.wait_ge(x2_ready, c + 1)
                    moments(xr[:, g * G:(g + 1) * G, :], 2 + c % 2, x2_var)
                if s < NG:
                    g = ORDER[s]
                    reciprocal(s % 2, hn_sd, s)
                    for y in range(G):
                        ins = nc.vector.tensor_scalar(eg[:, g * G + y, :], eg[:, g * G + y, :],
                                                      mv[:, s % 2, y, 0:1], rs[:, s % 2, y:y + 1],
                                                      ALU.subtract, ALU.mult)
                    ins.then_inc(hn_ready, 1)
                if 0 <= c < NG:
                    reciprocal(2 + c % 2, x2_sd, c)
                    if c >= 2:
                        dve.wait_ge(f_ready, c - 1)
                    neg_mean(c % 2, 2 + c % 2, x2_rs)
                c = s - 3
                if 0 <= c < NG:
                    g = ORDER[c]
                    dve.wait_ge(y_done, c + 1)
                    dve.wait_ge(f_ready, c + 1)
                    nc.vector.tensor_tensor(xr[:, g * G:(g + 1) * G, :],
                                            bank(TR + 1).rearrange("p (y d) -> p y d", d=D),
                                            xr[:, g * G:(g + 1) * G, :], ALU.add).then_inc(y_added, 1)

            def finish(k):
                row = xr[:, bass.ds(k, 1), :].rearrange("p k d -> p (k d)")
                nc.vector.scalar_tensor_tensor(out=row, in0=nacc(k), scalar=rdeg[:, bass.ds(k, 1)], in1=row,
                                               op0=ALU.mult, op1=ALU.add).then_inc(row_final, 1)

            dve.wait_ge(y_added, NG)

            def row_tile(k, j):
                dve.wait_ge(row_done, k - 1)
                unit(k, 0, j)
                finish(k - 2)
                for R in range(1, 4):
                    unit(k, R, j)

            for k in (2, 3):
                row_tile(k, k)
            with dve.Fori(1, NT // BT) as i:
                for j in range(BT):
                    row_tile(i * BT + j, j)
            for k in (NT - 2, NT - 1):
                dve.wait_ge(row_done, k + 1)
                finish(k)


_INS = ['x', 'adj', 'L0_gnn_W_u', 'L0_gnn_diag_u', 'L0_gnn_par_u', 'L0_gnn_W_i', 'L0_gnn_diag_i',
        'L0_gnn_par_i', 'L0_gnn_ln_gamma', 'L0_gnn_ln_beta', 'L1_gnn_W']


def kernel(**inputs):
    import numpy as _np
    import concourse.bacc as _bacc
    from concourse import mybir as _mybir
    from concourse.bass_utils import run_bass_kernel_spmd as _run

    nc = _bacc.Bacc("TRN2", target_bir_lowering=False, num_devices=1)
    arrays, args = {}, []
    for name in _INS:
        a = _np.ascontiguousarray(inputs[name])
        arrays[f"in_{name}"] = a
        args.append(nc.dram_tensor(f"in_{name}", a.shape, _mybir.dt.from_np(a.dtype), kind="ExternalInput").ap())
    args.append(nc.dram_tensor("out", (N, D), _mybir.dt.float32, kind="ExternalOutput").ap())
    build(nc, *args)
    r = _run(nc, [arrays], core_ids=[0])
    return r.results[0]["out"]
```

```python
from contextlib import ExitStack

import concourse.bass as bass
from concourse import mybir

F32 = mybir.dt.float32
F32R = mybir.dt.float32r
BF16 = mybir.dt.bfloat16
ALU = mybir.AluOpType
ACT = mybir.ActivationFunctionType
AX = mybir.AxisListType

P = 128
N = 5120
D = 64
EPS = 1e-5
NT = N // P
BANK = 512
W = 256
CB = W // P
NB = N // W
Y = BANK // P
NU = NT // Y
SLOTS = 5
G = BANK // D
NG = NT // G
UT = 2048 // P
SMALL = 14
IN_PSUM = [0, 2, 4, 6]
IN_SBUF = [g for g in range(NU) if g not in IN_PSUM]
NS = len(IN_SBUF)
RES = NB - 1
BU = NB - 1
LAG = 3
assert NU % SLOTS == 0 and NB % SLOTS == 0


def build(nc, x, adj, W_u, diag_u, par_u, W_i, diag_i, par_i, gamma, beta, W1, out):
    with ExitStack() as ctx:
        def sb(name, shape, dt=F32):
            return ctx.enter_context(nc.sbuf_tensor(name, shape, dt))

        def sem(name):
            return ctx.enter_context(nc.semaphore(name))

        kept = sb("kept", [P, 2, CB, N], F32R)
        nat = sb("nat", [P, SLOTS, Y, W])
        ring = sb("ring", [P, 4, 2, BANK], F32R)
        eg = sb("eg", [P, NT, 2, D], F32R)
        hT = sb("hT", [P, N])
        xr = sb("xr", [P, NT, D])
        h0 = sb("h0", [P, NT, D])
        tT = sb("tT", [P, W])
        th = sb("th", [P, CB, 2, D], F32R)
        yT = sb("yT", [P, BANK])
        ident = sb("ident", [P, P])
        twoid = sb("twoid", [P, D])
        zeros = sb("zeros", [P, BANK], BF16)
        degp = sb("degp", [P, NT, NB])
        rdeg = sb("rdeg", [P, 3, NT])
        dtab = sb("dtab", [NT, P])
        coef = sb("coef", [P, NT])
        par = sb("par", [P, 2, 2])
        parp = sb("parp", [P, 2])
        wui = sb("wui", [P, 2, 2, D])
        wst = sb("wst", [P, 4, P])
        wbd = sb("wbd", [P, 2, 2, D])
        gam = sb("gam", [P, D])
        bet = sb("bet", [P, D])
        eps = sb("eps", [P, 1])
        fb = sb("fb", [P, 2, G, D])
        fT = sb("fT", [P, G // 2, P])
        st = sb("st", [P, 4, G, 6])
        mv = sb("mv", [P, 4, G, 2])
        sd = sb("sd", [P, 4, G])
        rs = sb("rs", [P, 4, G])
        nm = sb("nm", [P, 2, G])

        ps = ctx.enter_context(nc.psum_tensor("ps", [P, 8 * BANK], F32))
        ACC, TB, TR = 4, 5, 6
        YG, HB, FB = 2, 5, 7
        BACC, BFIN = 4, 6

        def bank(b, n=BANK):
            return ps[:, b * BANK:b * BANK + n]

        def tiles(b, n=G):
            return bank(b, n * D).rearrange("p (y d) -> p y d", d=D)

        yg = ps[:, YG * BANK:(YG + 2) * BANK].rearrange("p (y m d) -> p y m d", m=2, d=D)

        x_landed = [sem(f"x_landed{g}") for g in range(NG)]
        small_landed = sem("small_landed")
        landed = [sem(f"landed{s}") for s in range(SLOTS)]
        stored = sem("stored")
        zeroed = sem("zeroed")
        consts = sem("consts")
        tabs_T = sem("tabs_T")
        tabs = sem("tabs")
        vec = sem("vec")
        pool_own = sem("pool_own")
        h0_var = sem("h0_var")
        h0_sd = sem("h0_sd")
        h0_rs = sem("h0_rs")
        h0_ready = sem("h0_ready")
        h0_T = sem("h0_T")
        h0T_ready = sem("h0T_ready")
        hw_done = sem("hw_done")
        ef_ready = sem("ef_ready")
        eh_ready = sem("eh_ready")
        e_ready = sem("e_ready")
        xrb_ready = sem("xrb_ready")
        nat_h = sem("nat_h")
        nat_l = sem("nat_l")
        t_summed = sem("t_summed")
        t_copied = sem("t_copied")
        t_turned = sem("t_turned")
        t_high = sem("t_high")
        t_ready = sem("t_ready")
        h_summed = sem("h_summed")
        h_added = sem("h_added")
        h_copied = sem("h_copied")
        piece_T = sem("piece_T")
        piece_h = sem("piece_h")
        piece_l = sem("piece_l")
        h_turned = sem("h_turned")
        hn_var = sem("hn_var")
        hn_sd = sem("hn_sd")
        hn_ready = sem("hn_ready")
        x2_ready = sem("x2_ready")
        x2_var = sem("x2_var")
        x2_sd = sem("x2_sd")
        x2_rs = sem("x2_rs")
        f_ready = sem("f_ready")
        f_T = sem("f_T")
        fT_ready = sem("fT_ready")
        y_done = sem("y_done")
        gh_ready = sem("gh_ready")
        g_ready = sem("g_ready")
        b_T = sem("b_T")
        b_h = sem("b_h")
        b_l = sem("b_l")
        b_used = sem("b_used")
        y_copied = sem("y_copied")
        y_turned = sem("y_turned")
        y_scaled = sem("y_scaled")
        final = sem("final")

        block = ctx.enter_context(nc.Block())

        def landed_a(i, g):
            return (i * (NU // SLOTS) + g // SLOTS + 1) * 16

        def landed_b(r, u):
            per = NB // SLOTS - (u % SLOTS == SLOTS - 1)
            return (NB * NU // SLOTS + r * per + u // SLOTS + 1) * 16

        def unit_source(rows, cols):
            return adj[rows, cols].rearrange("(y p) c -> p y c", p=P)

        @block.sync
        def _(sp):
            for g in range(NG):
                sp.dma_start(xr[:, g * G:(g + 1) * G, :],
                             x[g * G * P:(g + 1) * G * P, :].rearrange("(k p) d -> p k d", p=P)).then_inc(x_landed[g], 16)

            def load_a(i, g, cols):
                if not (isinstance(i, int) and i == 0 and g < SLOTS):
                    sp.wait_ge(piece_T, (i * NU + g - SLOTS + 1) * CB)
                sp.dma_start(nat[:, g % SLOTS], unit_source(slice(g * Y * P, (g + 1) * Y * P), cols)
                             ).then_inc(landed[g % SLOTS], 16)

            def load_b(r, u, rows):
                if isinstance(r, int) and r == 0 and u < SLOTS:
                    sp.wait_ge(piece_T, (NB * NU + u - SLOTS + 1) * CB)
                elif u < SLOTS:
                    before = u + NB - SLOTS if u < SLOTS - 1 else u + NB - 2 * SLOTS
                    sp.wait_ge(b_T, (r * BU - BU + before + 1) * CB)
                else:
                    sp.wait_ge(b_T, (r * BU + u - SLOTS + 1) * CB)
                sp.dma_start(nat[:, u % SLOTS], unit_source(rows, slice(u * W, (u + 1) * W))
                             ).then_inc(landed[u % SLOTS], 16)

            for g in range(NU):
                load_a(0, g, slice(0, W))
            with sp.Fori(1, NB) as i:
                for g in range(NU):
                    load_a(i, g, bass.ds(i * W, W))
            for u in range(BU):
                load_b(0, u, slice(0, Y * P))
            with sp.Fori(1, NU) as r:
                for u in range(BU):
                    load_b(r, u, bass.ds(r * (Y * P), Y * P))

        @block.gpsimd
        def _(pool):
            nc.gpsimd.memset(ident[:], 0.0).then_inc(pool_own, 1)
            nc.gpsimd.memset(twoid[:], 0.0).then_inc(pool_own, 1)
            nc.gpsimd.memset(zeros[:], 0.0).then_inc(consts, 1)
            nc.gpsimd.memset(eps[:], EPS).then_inc(consts, 1)
            pool.wait_ge(pool_own, 2)
            nc.gpsimd.affine_select(out=ident[:], in_=ident[:], compare_op=ALU.not_equal, fill=1.0, base=0,
                                    pattern=[[-1, P]], channel_multiplier=1).then_inc(consts, 1)
            nc.gpsimd.affine_select(out=twoid[:], in_=twoid[:], compare_op=ALU.not_equal, fill=1.0, base=0,
                                    pattern=[[-1, D]], channel_multiplier=1).then_inc(pool_own, 1)
            pool.wait_ge(pool_own, 3)
            nc.gpsimd.affine_select(out=twoid[:], in_=twoid[:], compare_op=ALU.not_equal, fill=1.0, base=-D,
                                    pattern=[[-1, D]], channel_multiplier=1).then_inc(consts, 1)
            nc.gpsimd.memset(hT[:], 0.0).then_inc(consts, 1)
            own = 3

            def low(i, g):
                for p in range(2):
                    pool.wait_ge(nat_h, (i * NU + g) * 2 + p + 1)
                    a = (2 * g + p) % 4
                    nc.gpsimd.tensor_tensor(ring[:, a, 1, :].rearrange("p (y c) -> p y c", y=2),
                                            nat[:, g % SLOTS, 2 * p:2 * p + 2, :],
                                            ring[:, a, 0, :].bitcast(F32).rearrange("p (y c) -> p y c", y=2),
                                            ALU.subtract).then_inc(nat_l, 1)

            for g in range(NU):
                low(0, g)
            pool.wait_ge(small_landed, 16 * SMALL)
            for g in range(NG):
                ks = slice(g * G, g * G + G)
                pool.wait_ge(h0_ready, g + 1)
                nc.gpsimd.tensor_tensor(xr[:, ks, :], xr[:, ks, :], h0[:, ks, :], ALU.add).then_inc(pool_own, 1)
                own += 1
                low(1, 2 * g)
                low(1, 2 * g + 1)
                pool.wait_ge(pool_own, own)
                nc.gpsimd.tensor_tensor(xr[:, ks, :], xr[:, ks, :], bet[:].unsqueeze(1).to_broadcast([P, G, D]),
                                        ALU.add).then_inc(xrb_ready, 1)
            with pool.Fori(2, NB) as i:
                for g in range(NU):
                    low(i, g)
            pool.wait_ge(xrb_ready, NG)
            for c in range(NG):
                ks = slice(c * G, c * G + G)
                pool.wait_ge(hn_ready, c + 1)
                nc.gpsimd.tensor_tensor(h0[:, ks, :], h0[:, ks, :], gam[:].unsqueeze(1).to_broadcast([P, G, D]),
                                        ALU.mult).then_inc(pool_own, 1)
                own += 1
                pool.wait_ge(pool_own, own)
                nc.gpsimd.tensor_tensor(xr[:, ks, :], xr[:, ks, :], h0[:, ks, :], ALU.add).then_inc(x2_ready, 1)

        @block.tensor
        def _(pe):
            pe.wait_ge(consts, 5)
            pe.wait_ge(small_landed, 16 * SMALL)
            nc.tensor.transpose(bank(0, NT), dtab[:], ident[0:NT, 0:NT])
            for s in range(4):
                mm = nc.tensor.transpose(bank(1)[:, s * P:(s + 1) * P], wst[:, s, :], ident[:])
            mm.then_inc(tabs_T, 1)

            def e_group(g):
                pe.wait_ge(h0_ready, g + 1)
                if g >= 1:
                    pe.wait_ge(h0T_ready, g)
                for y in range(G // 2):
                    mm = nc.tensor.transpose(bank(2)[:, y * P:(y + 1) * P], h0[:, g * G + 2 * y:g * G + 2 * y + 2, :],
                                             ident[:])
                mm.then_inc(h0_T, 1)
                pe.wait_ge(h0T_ready, g + 1)
                if g >= 1:
                    pe.wait_ge(ef_ready, g)
                who = 0 if g * G < UT else 1
                for y in range(G):
                    mm = nc.tensor.matmul(bank(3)[:, y * D:(y + 1) * D], fT[:, y // 2, :], wui[:, who, y % 2, :],
                                          start=True, stop=True)
                mm.then_inc(hw_done, 1)

            def sum_t(i, g):
                n = i * NU + g
                if g == 0 and not (isinstance(i, int) and i == 0):
                    pe.wait_ge(t_copied, i)
                for y in range(Y):
                    if y % 2 == 0:
                        pe.wait_ge(nat_l, n * 2 + y // 2 + 1)
                    a = (2 * g + y // 2) % 4
                    for s in range(2):
                        mm = nc.tensor.matmul(bank(TB, W), eg[:, g * Y + y, :, :], ring[:, a, s, (y % 2) * W:(y % 2 + 1) * W],
                                              start=(g == 0 and y == 0 and s == 0),
                                              stop=(g == NU - 1 and y == Y - 1 and s == 1), skip_group_check=True)
                mm.then_inc(t_summed, 1)

            def turn_t(i):
                pe.wait_ge(t_copied, i + 1)
                if not (isinstance(i, int) and i == 0):
                    pe.wait_ge(h_added, i * NS)
                for c in range(CB):
                    mm = nc.tensor.matmul(bank(ACC)[:, c * D:(c + 1) * D], tT[:, c * P:(c + 1) * P], twoid[:],
                                          start=True, stop=True)
                mm.then_inc(t_turned, 1)

            def sum_h(i, g):
                n = i * NU + g
                pe.wait_ge(piece_l, (n + 1) * CB)
                if g == 0:
                    pe.wait_ge(t_ready, i + 1)
                if g in IN_PSUM:
                    to = bank(IN_PSUM.index(g))
                else:
                    to = bank(ACC)
                    if IN_SBUF.index(g) > 0:
                        pe.wait_ge(h_added, i * NS + IN_SBUF.index(g))
                for c in range(CB):
                    for s in range(2):
                        mm = nc.tensor.matmul(to, th[:, c, :, :], kept[:, s, c, g * BANK:(g + 1) * BANK],
                                              start=(g in IN_SBUF and c == 0 and s == 0),
                                              stop=(g in IN_SBUF and c == CB - 1 and s == 1), skip_group_check=True)
                mm.then_inc(h_summed, 1)

            def turn_unit(i, g):
                n = i * NU + g
                for c in range(CB):
                    if not (isinstance(i, int) and n == 0):
                        pe.wait_ge(piece_l, (n - 1) * CB + c + 1)
                    for y in range(Y):
                        mm = nc.tensor.transpose(bank(TR + c)[:, y * P:(y + 1) * P],
                                                 nat[:, g % SLOTS, y, c * P:(c + 1) * P], ident[:])
                    mm.then_inc(piece_T, 1)

            def block_steps(i):
                for g in range(NU):
                    sum_t(i, g)
                    sum_h(i - 1, g)
                    turn_unit(i, g)
                turn_t(i)

            e_group(0)
            for g in range(NU):
                if g % 2 == 0:
                    pe.wait_ge(e_ready, g // 2 + 1)
                sum_t(0, g)
                turn_unit(0, g)
                if g % 2 == 0 and g // 2 + 1 < NG:
                    e_group(g // 2 + 1)
            turn_t(0)
            pe.wait_ge(tabs, 3)
            pe.wait_ge(ef_ready, NG)
            for b in range(len(IN_PSUM)):
                nc.tensor.matmul(bank(b), zeros[:, 0:P], zeros[:], start=True, stop=False, skip_group_check=True)
            with pe.Fori(1, NB) as i:
                block_steps(i)
            def turn_h(c):
                units = range((c + 1) * G // Y)
                pe.wait_ge(h_copied, len([g for g in units if g in IN_PSUM]))
                pe.wait_ge(h_added, (NB - 1) * NS + len([g for g in units if g in IN_SBUF]))
                if c >= 2:
                    pe.wait_ge(hn_ready, c - 1)
                elif c == 1:
                    pe.wait_ge(piece_l, NB * NU * CB)
                for y in range(G):
                    k = c * G + y
                    mm = nc.tensor.matmul(bank(HB + c % 2)[:, y * D:(y + 1) * D], hT[:, k * P:(k + 1) * P], twoid[:],
                                          start=True, stop=True)
                mm.then_inc(h_turned, 1)

            def g_group(c):
                pe.wait_ge(f_ready, c + 1)
                if c >= 1:
                    pe.wait_ge(fT_ready, c)
                for y in range(G // 2):
                    mm = nc.tensor.transpose(bank(FB)[:, y * P:(y + 1) * P], fb[:, c % 2, 2 * y:2 * y + 2, :], ident[:])
                mm.then_inc(f_T, 1)
                pe.wait_ge(fT_ready, c + 1)
                if c >= 1:
                    pe.wait_ge(g_ready, c)
                else:
                    pe.wait_ge(h_copied, len(IN_PSUM))
                for y in range(G):
                    mm = nc.tensor.matmul(ps[:, YG * BANK + y * P:YG * BANK + (y + 1) * P], fT[:, y // 2, :],
                                          wbd[:, y % 2, :, :], start=True, stop=True)
                mm.then_inc(y_done, 1)

            def b_turn(r, u):
                pe.wait_ge(landed[u % SLOTS], landed_b(r, u))
                first = isinstance(r, int) and r == 0
                for c in range(CB):
                    m = u * CB + c
                    back = 2 if first else 4
                    if first and m < 2:
                        pe.wait_ge(h_copied, len(IN_PSUM))
                    elif first:
                        pe.wait_ge(b_l, m - back + 1)
                    else:
                        pe.wait_ge(b_l, r * (BU * CB) + (m - back + 1))
                    for y in range(Y):
                        mm = nc.tensor.transpose(bank(m % back)[:, y * P:(y + 1) * P],
                                                 nat[:, u % SLOTS, y, c * P:(c + 1) * P], ident[:])
                    mm.then_inc(b_T, 1)

            def b_acc(r):
                if isinstance(r, int):
                    return bank(BACC + r % 2)
                return ps[:, bass.ds((r % 2) * BANK + BACC * BANK, BANK)]

            def b_sum(r, u):
                pe.wait_ge(b_l, r * (BU * CB) + (u + 1) * CB)
                for c in range(CB):
                    for s in range(2):
                        mm = nc.tensor.matmul(b_acc(r), eg[:, u * CB + c, :, :], ring[:, (u * CB + c) % 4, s, :],
                                              start=(u == 0 and c == 0 and s == 0), stop=(u == BU - 1 and c == CB - 1 and s == 1),
                                              skip_group_check=True)
                mm.then_inc(b_used, 1)

            def b_kept(r):
                for c in range(CB):
                    for s in range(2):
                        rows = slice(r * BANK, (r + 1) * BANK) if isinstance(r, int) else bass.ds(r * BANK, BANK)
                        nc.tensor.matmul(b_acc(r), eg[:, RES * CB + c, :, :], kept[:, s, c, rows],
                                         start=False, stop=False, skip_group_check=True)

            def b_finish(r):
                pe.wait_ge(y_copied, r + 1)
                if not (isinstance(r, int) and r == 0):
                    pe.wait_ge(y_scaled, r)
                for y in range(Y):
                    mm = nc.tensor.matmul(bank(BFIN)[:, y * D:(y + 1) * D], yT[:, y * P:(y + 1) * P], twoid[:],
                                          start=True, stop=True)
                mm.then_inc(y_turned, 1)

            for g in range(Y):
                sum_h(NB - 1, g)
            for s in range(NG + LAG + 1):
                if s < NG:
                    turn_h(s)
                    for g in range(Y + 2 * s, min(Y + 2 * s + 2, NU)):
                        sum_h(NB - 1, g)
                if 0 <= s - LAG < NG:
                    g_group(s - LAG)
                if s > LAG:
                    pe.wait_ge(g_ready, s - LAG)
                    for u in range((s - LAG - 1) * 4, min((s - LAG) * 4, BU)):
                        b_turn(0, u)
                        if u >= 1:
                            b_sum(0, u - 1)
            b_kept(0)
            b_sum(0, BU - 1)
            with pe.Fori(1, NU) as r:
                for u in range(BU):
                    b_turn(r, u)
                    if u >= 1:
                        b_sum(r, u - 1)
                    if u == 3:
                        b_finish(r - 1)
                b_kept(r)
                b_sum(r, BU - 1)
            b_finish(NU - 1)

        @block.scalar
        def _(act):
            def small(dst, src):
                act.dma_start(dst, src).then_inc(small_landed, 16)

            small(dtab[0:UT, :], diag_u.rearrange("(k p) -> k p", p=P))
            small(dtab[UT:NT, :], diag_i.rearrange("(k p) -> k p", p=P))
            small(par[:, 0, :], par_u.partition_broadcast(P))
            small(par[:, 1, :], par_i.partition_broadcast(P))
            small(gam[:], gamma.partition_broadcast(P))
            small(bet[:], beta.partition_broadcast(P))
            act.wait_ge(zeroed, 2)
            for s, w in enumerate((W_u, W_i)):
                small(wui[0:D, s, 0, :], w)
                small(wui[D:P, s, 1, :], w)
            for s in range(2):
                small(wst[0:D, 2 * s, 0:D], W1[:, s * D:(s + 1) * D])
                small(wst[0:D, 2 * s + 1, D:P], W1[:, s * D:(s + 1) * D])
            act.wait_ge(consts, 5)

            def h0_std(g):
                act.wait_ge(h0_var, g + 1)
                nc.scalar.activation(sd[:, g % 2, :], mv[:, g % 2, :, 1], ACT.Sqrt, bias=eps[:]).then_inc(h0_sd, 1)

            def h0_relu(g):
                act.wait_ge(h0_rs, g + 1)
                for y in range(G):
                    a = nc.scalar.activation(h0[:, g * G + y, :], xr[:, g * G + y, :], ACT.Relu,
                                             bias=nm[:, g % 2, y:y + 1], scale=rs[:, g % 2, y:y + 1])
                a.then_inc(h0_ready, 1)

            def h0T_copy(g):
                act.wait_ge(h0_T, g + 1)
                if g >= 1:
                    act.wait_ge(hw_done, g)
                nc.scalar.copy(fT[:], bank(2).rearrange("p (y r) -> p y r", r=P)).then_inc(h0T_ready, 1)

            def e_high(g):
                act.wait_ge(ef_ready, g + 1)
                nc.scalar.copy(eg[:, g * G:(g + 1) * G, 0, :], fb[:, g % 2, :, :]).then_inc(eh_ready, 1)

            def high(i, g):
                act.wait_ge(landed[g % SLOTS], landed_a(i, g))
                if not (isinstance(i, int) and i == 0 and g < 2):
                    act.wait_ge(t_summed, i * NU + g - 1)
                for y in range(Y):
                    a = (2 * g + y // 2) % 4
                    ins = nc.scalar.activation(ring[:, a, 0, (y % 2) * W:(y % 2 + 1) * W], nat[:, g % SLOTS, y, :],
                                               ACT.Copy, accum_out=degp[:, g * Y + y, bass.ds(i, 1)])
                    if y % 2 == 1:
                        ins.then_inc(nat_h, 1)

            def keep_high(i, g):
                for c in range(CB):
                    act.wait_ge(piece_T, (i * NU + g) * CB + c + 1)
                    nc.scalar.copy(kept[:, 0, c, g * BANK:(g + 1) * BANK], bank(TR + c)).then_inc(piece_h, 1)

            def copy_t(i):
                act.wait_ge(t_summed, (i + 1) * NU)
                if not (isinstance(i, int) and i == 0):
                    act.wait_ge(t_turned, i)
                nc.scalar.copy(tT[:], bank(TB, W)).then_inc(t_copied, 1)

            def t_split(i):
                act.wait_ge(t_turned, i + 1)
                nc.scalar.copy(th[:, :, 0, :], tiles(ACC, CB)).then_inc(t_high, 1)

            def block_steps(i, more=True):
                for g in range(NU):
                    if g < NU - 2:
                        high(i, g + 2)
                    elif more:
                        high(i + 1, g + 2 - NU)
                    if g == NU - 1:
                        copy_t(i)
                    keep_high(i, g)
                t_split(i)

            h0_std(0)
            h0_relu(0)
            h0_std(1)
            h0T_copy(0)
            high(0, 0)
            e_high(0)
            h0_relu(1)
            high(0, 1)
            for g in range(NU):
                high(*((0, g + 2) if g < NU - 2 else (1, g + 2 - NU)))
                if g == NU - 1:
                    copy_t(0)
                keep_high(0, g)
                if g % 2 == 0 and g // 2 + 1 < NG:
                    h0T_copy(g // 2 + 1)
                    if g // 2 + 2 < NG:
                        h0_std(g // 2 + 2)
                        h0_relu(g // 2 + 2)
                    e_high(g // 2 + 1)
            t_split(0)
            with act.Fori(1, NB - 1) as i:
                block_steps(i)
            block_steps(NB - 1, more=False)
            for b, g in enumerate(IN_PSUM):
                act.wait_ge(h_summed, (NB - 1) * NU + g + 1)
                nc.scalar.copy(hT[:, g * BANK:(g + 1) * BANK], bank(b)).then_inc(h_copied, 1)

            def std(c, which, have, give):
                act.wait_ge(have, c + 1)
                nc.scalar.activation(sd[:, which, :], mv[:, which, :, 1], ACT.Sqrt, bias=eps[:]).then_inc(give, 1)

            def b_high(r, u):
                first = isinstance(r, int) and r == 0
                back = 2 if first else 4
                if not (first and u < 2):
                    act.wait_ge(b_used, r * BU + u - 1)
                for c in range(CB):
                    m = u * CB + c
                    act.wait_ge(b_T, r * (BU * CB) + m + 1)
                    nc.scalar.copy(ring[:, m % 4, 0, :], bank(m % back)).then_inc(b_h, 1)

            for s in range(NG + LAG + 1):
                c = s - LAG
                if 0 <= c < NG:
                    act.wait_ge(f_T, c + 1)
                    if c >= 1:
                        act.wait_ge(y_done, c)
                    nc.scalar.copy(fT[:], bank(FB).rearrange("p (y r) -> p y r", r=P)).then_inc(fT_ready, 1)
                if s < NG:
                    std(s, s % 2, hn_var, hn_sd)
                c = s - 2
                if 0 <= c < NG:
                    std(c, 2 + c % 2, x2_var, x2_sd)
                    act.wait_ge(x2_rs, c + 1)
                    if c >= 2:
                        act.wait_ge(f_T, c - 1)
                    for y in range(G):
                        a = nc.scalar.activation(fb[:, c % 2, y, :], xr[:, c * G + y, :], ACT.Relu,
                                                 bias=nm[:, c % 2, y:y + 1], scale=rs[:, 2 + c % 2, y:y + 1])
                    a.then_inc(f_ready, 1)
                c = s - LAG
                if 0 <= c < NG:
                    act.wait_ge(y_done, c + 1)
                    nc.scalar.copy(eg[:, c * G:(c + 1) * G, 0, :], yg[:, :, 1, :]).then_inc(gh_ready, 1)
                if s > LAG:
                    for u in range((s - LAG - 1) * 4, min((s - LAG) * 4, BU)):
                        b_high(0, u)

            def copy_y(r):
                act.wait_ge(b_used, (r + 1) * BU)
                if not (isinstance(r, int) and r == 0):
                    act.wait_ge(y_turned, r)
                src = bank(BACC + r % 2) if isinstance(r, int) else ps[:, bass.ds((r % 2) * BANK + BACC * BANK, BANK)]
                nc.scalar.copy(yT[:], src).then_inc(y_copied, 1)

            def store(r):
                act.wait_ge(final, r + 1)
                rows = slice(r * BANK, (r + 1) * BANK) if isinstance(r, int) else bass.ds(r * BANK, BANK)
                ks = slice(r * Y, (r + 1) * Y) if isinstance(r, int) else bass.ds(r * Y, Y)
                act.dma_start(out[rows, :].rearrange("(y p) d -> p y d", p=P), xr[:, ks, :]).then_inc(stored, 16)

            with act.Fori(1, NU) as r:
                for u in range(BU):
                    b_high(r, u)
                    if u == 1:
                        copy_y(r - 1)
                    if u == 12:
                        store(r - 1)
            copy_y(NU - 1)
            store(NU - 1)
            act.wait_ge(stored, 16 * NU)

        @block.vector
        def _(dve):
            own = [0]

            def link(ins):
                own[0] += 1
                ins.then_inc(vec, 1)
                dve.wait_ge(vec, own[0])

            nc.vector.memset(wui[:], 0.0).then_inc(zeroed, 1)
            nc.vector.memset(wst[:], 0.0).then_inc(zeroed, 1)

            def moments(src, which, give):
                for y in range(G):
                    ins = nc.vector.bn_stats(st[:, which, y, :], src[:, y, :])
                link(ins)
                for y in range(G):
                    ins = nc.vector.bn_aggr(mv[:, which, y, :], st[:, which, y, :])
                ins.then_inc(give, 1)

            def reciprocal(which, have, c):
                dve.wait_ge(have, c + 1)
                link(nc.vector.reciprocal(rs[:, which, :], sd[:, which, :]))

            def neg_mean(slot, which, give):
                nc.vector.scalar_tensor_tensor(out=nm[:, slot, :], in0=mv[:, which, :, 0], scalar=-1.0,
                                               in1=rs[:, which, :], op0=ALU.mult, op1=ALU.mult).then_inc(give, 1)

            def h0_moments(g):
                dve.wait_ge(x_landed[g], 16)
                if g >= 2:
                    dve.wait_ge(h0_ready, g - 1)
                moments(xr[:, g * G:(g + 1) * G, :], g % 2, h0_var)

            def h0_scale(g):
                reciprocal(g % 2, h0_sd, g)
                neg_mean(g % 2, g % 2, h0_rs)

            def make_e(g):
                ks = slice(g * G, (g + 1) * G)
                dve.wait_ge(hw_done, g + 1)
                dve.wait_ge(h0_ready, g + 1)
                e = fb[:, g % 2, :, :]
                link(nc.vector.tensor_tensor(e, tiles(3), coef[:, ks].unsqueeze(2).to_broadcast([P, G, D]), ALU.mult))
                nc.vector.tensor_tensor(e, e, h0[:, ks, :], ALU.add).then_inc(ef_ready, 1)
                dve.wait_ge(ef_ready, g + 1)
                dve.wait_ge(eh_ready, g + 1)
                nc.vector.tensor_tensor(eg[:, ks, 1, :], e, eg[:, ks, 0, :].bitcast(F32), ALU.subtract
                                        ).then_inc(e_ready, 1)

            def keep_low(i, g):
                for c in range(CB):
                    dve.wait_ge(piece_h, (i * NU + g) * CB + c + 1)
                    to = slice(g * BANK, (g + 1) * BANK)
                    nc.vector.tensor_tensor(kept[:, 1, c, to], bank(TR + c), kept[:, 0, c, to].bitcast(F32),
                                            ALU.subtract).then_inc(piece_l, 1)

            def add_h(i, g):
                if g not in IN_SBUF:
                    return
                dve.wait_ge(h_summed, i * NU + g + 1)
                to = hT[:, g * BANK:(g + 1) * BANK]
                nc.vector.tensor_tensor(to, bank(ACC), to, ALU.add).then_inc(h_added, 1)

            def t_split(i):
                dve.wait_ge(t_high, i + 1)
                nc.vector.tensor_tensor(th[:, :, 1, :], tiles(ACC, CB), th[:, :, 0, :].bitcast(F32), ALU.subtract
                                        ).then_inc(t_ready, 1)

            def block_steps(i):
                for g in range(NU):
                    add_h(i - 1, g)
                    keep_low(i, g)
                t_split(i)

            h0_moments(0)
            h0_moments(1)
            h0_scale(0)
            h0_scale(1)
            dve.wait_ge(small_landed, 16 * SMALL)
            link(nc.vector.tensor_tensor(parp[:], par[:, :, 0], par[:, :, 1], ALU.mult))
            dve.wait_ge(tabs_T, 1)
            nc.vector.tensor_copy(wbd[:].rearrange("p h m d -> p m h d"),
                                  bank(1).rearrange("p (m h c) -> p m h c", m=2, c=P)[:, :, :, 0:D]).then_inc(tabs, 1)
            nc.vector.tensor_scalar(coef[:, 0:UT], bank(0, UT), parp[:, 0:1], None, ALU.mult).then_inc(tabs, 1)
            nc.vector.tensor_scalar(coef[:, UT:NT], bank(0, NT)[:, UT:NT], parp[:, 1:2], None, ALU.mult
                                    ).then_inc(tabs, 1)
            dve.wait_ge(tabs, 3)
            make_e(0)
            for g in range(NU):
                keep_low(0, g)
                if g % 2 == 0 and g // 2 + 2 < NG:
                    h0_moments(g // 2 + 2)
                    h0_scale(g // 2 + 2)
                if g % 2 == 0 and g // 2 + 1 < NG:
                    make_e(g // 2 + 1)
            t_split(0)
            with dve.Fori(1, NB) as i:
                block_steps(i)

            def b_low(r, u):
                back = 2 if isinstance(r, int) and r == 0 else 4
                for c in range(CB):
                    m = u * CB + c
                    dve.wait_ge(b_h, r * (BU * CB) + m + 1)
                    nc.vector.tensor_tensor(ring[:, m % 4, 1, :], bank(m % back), ring[:, m % 4, 0, :].bitcast(F32),
                                            ALU.subtract).then_inc(b_l, 1)

            dve.wait_ge(xrb_ready, NG)
            for g in range(Y):
                add_h(NB - 1, g)
            for s in range(NG + LAG + 1):
                if s < NG:
                    h = tiles(HB + s % 2)
                    dve.wait_ge(h_turned, s + 1)
                    moments(h, s % 2, hn_var)
                c = s - 2
                if 0 <= c < NG:
                    dve.wait_ge(x2_ready, c + 1)
                    moments(xr[:, c * G:(c + 1) * G, :], 2 + c % 2, x2_var)
                if s < NG:
                    reciprocal(s % 2, hn_sd, s)
                    for y in range(G):
                        ins = nc.vector.tensor_scalar(h0[:, s * G + y, :], h[:, y, :],
                                                      mv[:, s % 2, y, 0:1], rs[:, s % 2, y:y + 1],
                                                      ALU.subtract, ALU.mult)
                    ins.then_inc(hn_ready, 1)
                    for g in range(Y + 2 * s, min(Y + 2 * s + 2, NU)):
                        add_h(NB - 1, g)
                if 0 <= c < NG:
                    reciprocal(2 + c % 2, x2_sd, c)
                    if c >= 2:
                        dve.wait_ge(f_ready, c - 1)
                    neg_mean(c % 2, 2 + c % 2, x2_rs)
                c = s - LAG
                if 0 <= c < NG:
                    dve.wait_ge(gh_ready, c + 1)
                    ks = slice(c * G, (c + 1) * G)
                    nc.vector.tensor_tensor(eg[:, ks, 1, :], yg[:, :, 1, :], eg[:, ks, 0, :].bitcast(F32), ALU.subtract)
                    nc.vector.tensor_tensor(xr[:, ks, :], yg[:, :, 0, :], xr[:, ks, :], ALU.add).then_inc(g_ready, 1)
                if s > LAG:
                    for u in range((s - LAG - 1) * 4, min((s - LAG) * 4, BU)):
                        b_low(0, u)

            link(nc.vector.tensor_reduce(rdeg[:, 0, :], degp[:], AX.X, ALU.add))
            link(nc.vector.tensor_scalar(rdeg[:, 1, :], rdeg[:, 0, :], 1.0, None, ALU.add))
            link(nc.vector.reciprocal(rdeg[:, 2, :], rdeg[:, 1, :]))

            def finish(r):
                dve.wait_ge(y_turned, r + 1)
                ks = slice(r * Y, (r + 1) * Y) if isinstance(r, int) else bass.ds(r * Y, Y)
                if not (isinstance(r, int) and r == 0):
                    dve.wait_ge(final, r)
                v = fb[:, 0, 0:Y, :]
                nc.vector.tensor_tensor(v, tiles(BFIN, Y), rdeg[:, 2, ks].unsqueeze(2).to_broadcast([P, Y, D]),
                                        ALU.mult).then_inc(y_scaled, 1)
                dve.wait_ge(y_scaled, r + 1)
                nc.vector.tensor_tensor(xr[:, ks, :], v, xr[:, ks, :], ALU.add).then_inc(final, 1)

            with dve.Fori(1, NU) as r:
                for u in range(BU):
                    b_low(r, u)
                    if u == 8:
                        finish(r - 1)
            finish(NU - 1)


_INS = ['x', 'adj', 'L0_gnn_W_u', 'L0_gnn_diag_u', 'L0_gnn_par_u', 'L0_gnn_W_i', 'L0_gnn_diag_i',
        'L0_gnn_par_i', 'L0_gnn_ln_gamma', 'L0_gnn_ln_beta', 'L1_gnn_W']


def kernel(**inputs):
    import numpy as _np
    import concourse.bacc as _bacc
    from concourse import mybir as _mybir
    from concourse.bass_utils import run_bass_kernel_spmd as _run

    nc = _bacc.Bacc("TRN2", target_bir_lowering=False, num_devices=1)
    arrays, args = {}, []
    for name in _INS:
        a = _np.ascontiguousarray(inputs[name])
        arrays[f"in_{name}"] = a
        args.append(nc.dram_tensor(f"in_{name}", a.shape, _mybir.dt.from_np(a.dtype), kind="ExternalInput").ap())
    args.append(nc.dram_tensor("out", (N, D), _mybir.dt.float32, kind="ExternalOutput").ap())
    build(nc, *args)
    r = _run(nc, [arrays], core_ids=[0])
    return r.results[0]["out"]
```

```python
from contextlib import ExitStack

import concourse.bass as bass
from concourse import mybir

F32 = mybir.dt.float32
F32R = mybir.dt.float32r
BF16 = mybir.dt.bfloat16
ALU = mybir.AluOpType
ACT = mybir.ActivationFunctionType
AX = mybir.AxisListType

P = 128
N = 5120
D = 64
EPS = 1e-5
NT = N // P
BANK = 512
W = 256
CB = W // P
NB = N // W
Y = BANK // P
NU = NT // Y
SLOTS = 10
NAT_SLOTS = 5
LOADED_T = [3, 6, 9]
G = BANK // D
NG = NT // G
UT = 2048 // P
WUI = 0
WBD = WUI + 4 * D
DIAG = WBD + 4 * D
PAR = DIAG + NT
GAM = PAR + 4
BET = GAM + D
SMALL = BET + D
IN_PSUM = [0, 3, 6, 9]
IN_SBUF = [g for g in range(NU) if g not in IN_PSUM]
NS = len(IN_SBUF)
RES = NB - 1
BU = NB - 1
assert NU % NAT_SLOTS == 0 and NAT_SLOTS + len(LOADED_T) <= SLOTS and NB % SLOTS == 0 and 0 not in LOADED_T
assert NU % 2 == 0 and BU % 2 == 1


def build(nc, x, units, units_T, small, out):
    with ExitStack() as ctx:
        def sb(name, shape, dt=F32):
            return ctx.enter_context(nc.sbuf_tensor(name, shape, dt))

        def sem(name):
            return ctx.enter_context(nc.semaphore(name))

        kept = sb("kept", [P, 2, CB, N], F32R)
        nat = sb("nat", [P, SLOTS, Y * W])
        ring = sb("ring", [P, 4, 2, BANK], F32R)
        eg = sb("eg", [P, NT, 2, D], F32R)
        hT = sb("hT", [P, N])
        xr = sb("xr", [P, NT, D])
        tT = sb("tT", [P, W])
        th = sb("th", [P, CB, 2, D], F32R)
        yT = sb("yT", [P, BANK])
        ident = sb("ident", [P, P])
        twoid = sb("twoid", [P, D])
        zeros = sb("zeros", [P, BANK], BF16)
        degp = sb("degp", [P, NT, NB])
        rdeg = sb("rdeg", [P, 3, NT])
        coef = sb("coef", [P, NT])
        parp = sb("parp", [P, 2])
        sm = sb("sm", [P, SMALL])
        eps = sb("eps", [P, 1])
        first = sb("first", [P, 1])
        fb = sb("fb", [P, 2, G, D])
        fT = sb("fT", [P, G // 2, P])
        st = sb("st", [P, 4, G, 6])
        mv = sb("mv", [P, 4, G, 2])
        sd = sb("sd", [P, 4, G])
        rs = sb("rs", [P, 4, G])
        nm = sb("nm", [P, 2, G])

        wui = sm[:, WUI:WBD].rearrange("p (w h d) -> p w h d", w=2, h=2)
        wbd = sm[:, WBD:DIAG].rearrange("p (h m) -> p h m", h=2)
        par = sm[:, PAR:GAM].rearrange("p (w n) -> p w n", w=2)
        gam, bet = sm[:, GAM:BET], sm[:, BET:SMALL]
        h0 = hT[:, 0:NT * D].rearrange("p (k d) -> p k d", d=D)
        hn = hT[:].rearrange("p (c q) -> p c q", c=NG)[:, :, 0:G * D]
        hn = hn.rearrange("p c (y d) -> p c y d", d=D)

        ps = ctx.enter_context(nc.psum_tensor("ps", [P, 8 * BANK], F32))
        ACC, TB, TR = 4, 5, 6
        YG, HB, FB = 2, 5, 7
        BACC, BFIN = 0, 6

        def bank(b, n=BANK):
            return ps[:, b * BANK:b * BANK + n]

        def tiles(b, n=G):
            return bank(b, n * D).rearrange("p (y d) -> p y d", d=D)

        yg = ps[:, YG * BANK:(YG + 2) * BANK].rearrange("p (y m d) -> p y m d", m=2, d=D)

        x_landed = [sem(f"x_landed{g}") for g in range(NG)]
        small_landed = sem("small_landed")
        landed = [sem(f"landed{s}") for s in range(SLOTS)]
        stored = sem("stored")
        consts = sem("consts")
        vec = sem("vec")
        pool_own = sem("pool_own")
        h0_var = sem("h0_var")
        h0_sd = sem("h0_sd")
        h0_ready = sem("h0_ready")
        h0_T = sem("h0_T")
        h0T_ready = sem("h0T_ready")
        hw_done = sem("hw_done")
        ef_ready = sem("ef_ready")
        eh_ready = sem("eh_ready")
        e_ready = sem("e_ready")
        xrb_ready = sem("xrb_ready")
        nat_h = sem("nat_h")
        nat_l = sem("nat_l")
        t_summed = sem("t_summed")
        t_copied = sem("t_copied")
        t_turned = sem("t_turned")
        t_high = sem("t_high")
        t_ready = sem("t_ready")
        h_summed = sem("h_summed")
        h_added = sem("h_added")
        h_copied = sem("h_copied")
        piece_T = sem("piece_T")
        piece_h = [sem(f"piece_h{c}") for c in range(CB)]
        piece_l = sem("piece_l")
        h_turned = sem("h_turned")
        hn_var = sem("hn_var")
        hn_sd = sem("hn_sd")
        h_centred = sem("h_centred")
        x2_ready = sem("x2_ready")
        x2_var = sem("x2_var")
        x2_sd = sem("x2_sd")
        x2_rs = sem("x2_rs")
        f_ready = sem("f_ready")
        f_T = sem("f_T")
        fT_ready = sem("fT_ready")
        y_done = sem("y_done")
        gh_ready = sem("gh_ready")
        g_ready = sem("g_ready")
        b_h = sem("b_h")
        b_l = [sem(f"b_l{c}") for c in range(CB)]
        b_used = sem("b_used")
        y_summed = sem("y_summed")
        y_copied = sem("y_copied")
        y_turned = sem("y_turned")
        y_scaled = sem("y_scaled")
        final = sem("final")

        block = ctx.enter_context(nc.Block())

        def landed_a(i, g):
            return (i * (NU // NAT_SLOTS) + g // NAT_SLOTS + 1) * 16

        def slot_T(g):
            return NAT_SLOTS + LOADED_T.index(g)

        def landed_b(r, u):
            slot = u % SLOTS
            in_a = NB * NU // NAT_SLOTS if slot < NAT_SLOTS else NB if slot < NAT_SLOTS + len(LOADED_T) else 0
            per = NB // SLOTS - (slot == SLOTS - 1)
            return (in_a + r * per + u // SLOTS + 1) * 16

        def turned(i, g, c):
            before = len([u for u in range(g) if u not in LOADED_T])
            return (i * (NU - len(LOADED_T)) + before) * CB + c + 1

        def piece(g, c):
            return nat[:, slot_T(g), c * BANK:(c + 1) * BANK] if g in LOADED_T else bank(TR + c)

        def wait_piece(engine, i, g, c):
            if g in LOADED_T:
                engine.wait_ge(landed[slot_T(g)], (i + 1) * 16)
            else:
                engine.wait_ge(piece_T, turned(i, g, c))
            if (g == 0 or g in LOADED_T) and not (isinstance(i, int) and i == 0):
                engine.wait_ge(h_summed, (i - 1) * NU + g + 1)

        def rows_of(dram, n):
            return dram[n * P:(n + 1) * P, :] if isinstance(n, int) else dram[bass.ds(n * P, P), :]

        def parts(u, c):
            return ring[:, u % 2 * CB + c]

        def b_units(s):
            us = [u for u in range((s - 2) * 4, (s - 1) * 4) if 0 <= u < BU]
            return [us[n:n + 1] for n in range(4)]

        def h_units(s):
            return range(Y + 4 * s, min(Y + 4 * s + 4, NU))

        def row_groups(engine, steps):
            with engine.Fori(0, (NU - 2) // 2) as m:
                steps(2 * m + 1, 1)
                steps(2 * m + 2, 0)
            steps(NU - 1, 1)

        @block.sync
        def _(sp):
            def load_x(g):
                sp.dma_start(xr[:, g * G:(g + 1) * G, :], x[:, g * G:(g + 1) * G, :]).then_inc(x_landed[g], 16)

            def wait_slot(i, g):
                if g in LOADED_T:
                    sp.wait_ge(nat_l, (i * NU + g + 1) * 2)
                else:
                    sp.wait_ge(piece_T, turned(i, g, CB - 1))

            def load_a(i, g):
                if not (isinstance(i, int) and i == 0 and g < NAT_SLOTS):
                    wait_slot(*((i, g - NAT_SLOTS) if g >= NAT_SLOTS else (i - 1, g + NU - NAT_SLOTS)))
                slot = g % NAT_SLOTS
                sp.dma_start(nat[:, slot], rows_of(units, i * NU + g)).then_inc(landed[slot], 16)
                if g in LOADED_T:
                    if not (isinstance(i, int) and i == 0):
                        sp.wait_ge(piece_l, ((i - 1) * NU + g + 1) * CB)
                    sp.dma_start(nat[:, slot_T(g)], rows_of(units_T, g * NB + i)).then_inc(landed[slot_T(g)], 16)

            def load_b(r, u):
                if isinstance(r, int) and r == 0 and u < SLOTS:
                    if u < NAT_SLOTS:
                        wait_slot(NB - 1, u + NU - NAT_SLOTS)
                    elif u < NAT_SLOTS + len(LOADED_T):
                        sp.wait_ge(piece_l, ((NB - 1) * NU + LOADED_T[u - NAT_SLOTS] + 1) * CB)
                else:
                    back = SLOTS if u >= SLOTS else BU if u == SLOTS - 1 else BU - SLOTS
                    for c in range(CB):
                        sp.wait_ge(b_l[c], r * BU + u - back + 1)
                sp.dma_start(nat[:, u % SLOTS], rows_of(units_T, r * NB + u)).then_inc(landed[u % SLOTS], 16)

            load_x(0)
            sp.dma_start(sm[:], small).then_inc(small_landed, 16)
            load_a(0, 0)
            load_x(1)
            load_a(0, 1)
            load_x(2)
            load_a(0, 2)
            load_x(3)
            load_a(0, 3)
            load_x(4)
            for g in range(4, NU):
                load_a(0, g)
            with sp.Fori(1, NB) as i:
                for g in range(NU):
                    load_a(i, g)
            for u in range(BU):
                load_b(0, u)
            with sp.Fori(1, NU) as r:
                for u in range(BU):
                    load_b(r, u)

        @block.gpsimd
        def _(pool):
            nc.gpsimd.memset(ident[:], 0.0).then_inc(pool_own, 1)
            nc.gpsimd.memset(twoid[:], 0.0).then_inc(pool_own, 1)
            nc.gpsimd.memset(zeros[:], 0.0).then_inc(consts, 1)
            nc.gpsimd.memset(eps[:], EPS).then_inc(consts, 1)
            pool.wait_ge(pool_own, 2)
            nc.gpsimd.affine_select(out=ident[:], in_=ident[:], compare_op=ALU.not_equal, fill=1.0, base=0,
                                    pattern=[[-1, P]], channel_multiplier=1).then_inc(consts, 1)
            nc.gpsimd.affine_select(out=twoid[:], in_=twoid[:], compare_op=ALU.not_equal, fill=1.0, base=0,
                                    pattern=[[-1, D]], channel_multiplier=1).then_inc(pool_own, 1)
            pool.wait_ge(pool_own, 3)
            nc.gpsimd.affine_select(out=twoid[:], in_=twoid[:], compare_op=ALU.not_equal, fill=1.0, base=-D,
                                    pattern=[[-1, D]], channel_multiplier=1).then_inc(consts, 1)
            own = 3

            def low(i, g):
                for p in range(2):
                    pool.wait_ge(nat_h, (i * NU + g) * 2 + p + 1)
                    a = (2 * g + p) % 4
                    nc.gpsimd.tensor_tensor(ring[:, a, 1, :], nat[:, g % NAT_SLOTS, p * BANK:(p + 1) * BANK],
                                            ring[:, a, 0, :].bitcast(F32), ALU.subtract).then_inc(nat_l, 1)

            low(0, 0)
            low(0, 1)
            for n in range(2, 2 * NU):
                low(n // NU, n % NU)
            with pool.Fori(2, NB) as i:
                for g in range(NU):
                    low(i, g)
            pool.wait_ge(xrb_ready, NG)
            pool.wait_ge(small_landed, 16)

            def b_low(u):
                pool.wait_ge(b_h, u * CB + 2)
                nc.gpsimd.tensor_tensor(parts(u, 1)[:, 1, :], nat[:, u % SLOTS, BANK:2 * BANK],
                                        parts(u, 1)[:, 0, :].bitcast(F32), ALU.subtract).then_inc(b_l[1], 1)

            for s in range(NG + 2):
                first, *others = b_units(s)
                for u in first:
                    b_low(u)
                if s < NG:
                    ks = slice(s * G, s * G + G)
                    pool.wait_ge(h_centred, s + 1)
                    nc.gpsimd.tensor_tensor(hn[:, s], hn[:, s], rs[:, s % 2, :].unsqueeze(2).to_broadcast([P, G, D]),
                                            ALU.mult).then_inc(pool_own, 1)
                    pool.wait_ge(pool_own, own + 1)
                    nc.gpsimd.tensor_tensor(hn[:, s], hn[:, s], gam.unsqueeze(1).to_broadcast([P, G, D]),
                                            ALU.mult).then_inc(pool_own, 1)
                    own += 2
                    pool.wait_ge(pool_own, own)
                    nc.gpsimd.tensor_tensor(xr[:, ks, :], xr[:, ks, :], hn[:, s], ALU.add).then_inc(x2_ready, 1)
                for us in others:
                    for u in us:
                        b_low(u)

        @block.tensor
        def _(pe):
            pe.wait_ge(consts, 4)
            pe.wait_ge(small_landed, 16)

            def h0_turn(g):
                pe.wait_ge(h0_ready, g + 1)
                if g >= 1:
                    pe.wait_ge(h0T_ready, g)
                for y in range(G // 2):
                    mm = nc.tensor.transpose(bank(2)[:, y * P:(y + 1) * P], h0[:, g * G + 2 * y:g * G + 2 * y + 2, :],
                                             ident[:])
                mm.then_inc(h0_T, 1)

            def h0_w(g):
                pe.wait_ge(h0T_ready, g + 1)
                if g >= 1:
                    pe.wait_ge(ef_ready, g)
                who = 0 if g * G < UT else 1
                for y in range(G):
                    mm = nc.tensor.matmul(bank(3)[:, y * D:(y + 1) * D], fT[:, y // 2, :], wui[:, who, y % 2, :],
                                          start=True, stop=True)
                mm.then_inc(hw_done, 1)

            def sum_t(i, g):
                n = i * NU + g
                if g == 0 and not (isinstance(i, int) and i == 0):
                    pe.wait_ge(t_copied, i)
                for y in range(Y):
                    if y % 2 == 0:
                        pe.wait_ge(nat_l, n * 2 + y // 2 + 1)
                    a = (2 * g + y // 2) % 4
                    for s in range(2):
                        mm = nc.tensor.matmul(bank(TB, W), eg[:, g * Y + y, :, :], ring[:, a, s, (y % 2) * W:(y % 2 + 1) * W],
                                              start=(g == 0 and y == 0 and s == 0),
                                              stop=(g == NU - 1 and y == Y - 1 and s == 1), skip_group_check=True)
                mm.then_inc(t_summed, 1)

            def turn_t(i):
                pe.wait_ge(t_copied, i + 1)
                if not (isinstance(i, int) and i == 0):
                    pe.wait_ge(h_added, i * NS)
                for c in range(CB):
                    mm = nc.tensor.matmul(bank(ACC)[:, c * D:(c + 1) * D], tT[:, c * P:(c + 1) * P], twoid[:],
                                          start=True, stop=True)
                mm.then_inc(t_turned, 1)

            def sum_h(i, g):
                n = i * NU + g
                pe.wait_ge(piece_l, (n + 1) * CB)
                if g == 0:
                    pe.wait_ge(t_ready, i + 1)
                if g in IN_PSUM:
                    to = bank(IN_PSUM.index(g))
                else:
                    to = bank(ACC)
                    if IN_SBUF.index(g) > 0:
                        pe.wait_ge(h_added, i * NS + IN_SBUF.index(g))
                for c in range(CB):
                    for s in range(2):
                        mm = nc.tensor.matmul(to, th[:, c, :, :], kept[:, s, c, g * BANK:(g + 1) * BANK],
                                              start=(g in IN_SBUF and c == 0 and s == 0),
                                              stop=(g in IN_SBUF and c == CB - 1 and s == 1), skip_group_check=True)
                mm.then_inc(h_summed, 1)

            def turn_unit(i, g):
                if g in LOADED_T:
                    return
                last = i * NU + g - (2 if (g - 1) % NU in LOADED_T else 1)
                for c in range(CB):
                    if not (isinstance(i, int) and i == 0 and g == 0):
                        pe.wait_ge(piece_l, last * CB + c + 1)
                    for y in range(Y):
                        mm = nc.tensor.transpose(bank(TR + c)[:, y * P:(y + 1) * P],
                                                 nat[:, g % NAT_SLOTS, y * W + c * P:y * W + (c + 1) * P], ident[:])
                    mm.then_inc(piece_T, 1)

            def block_steps(i):
                for g in range(NU):
                    sum_t(i, g)
                    if g == 0:
                        turn_unit(i, g)
                        sum_h(i - 1, g)
                    else:
                        sum_h(i - 1, g)
                        turn_unit(i, g)
                turn_t(i)

            for g in range(2):
                h0_turn(g)
                h0_w(g)
            for k in range(NG):
                pe.wait_ge(e_ready, k + 1)
                sum_t(0, 2 * k)
                if k + 2 < NG:
                    h0_turn(k + 2)
                turn_unit(0, 2 * k)
                if k + 2 < NG:
                    h0_w(k + 2)
                sum_t(0, 2 * k + 1)
                turn_unit(0, 2 * k + 1)
            turn_t(0)
            pe.wait_ge(ef_ready, NG)
            for b in range(len(IN_PSUM)):
                nc.tensor.matmul(bank(b), zeros[:, 0:P], zeros[:], start=True, stop=False, skip_group_check=True)
            with pe.Fori(1, NB) as i:
                block_steps(i)
            def turn_h(c):
                units = range((c + 1) * G // Y)
                pe.wait_ge(h_copied, len([g for g in units if g in IN_PSUM]))
                pe.wait_ge(h_added, (NB - 1) * NS + len([g for g in units if g in IN_SBUF]))
                if c >= 2:
                    pe.wait_ge(h_centred, c - 1)
                elif c == 1:
                    pe.wait_ge(piece_l, NB * NU * CB)
                for y in range(G):
                    k = c * G + y
                    mm = nc.tensor.matmul(bank(HB + c % 2)[:, y * D:(y + 1) * D], hT[:, k * P:(k + 1) * P], twoid[:],
                                          start=True, stop=True)
                mm.then_inc(h_turned, 1)

            def f_turn(c):
                pe.wait_ge(f_ready, c + 1)
                if c >= 1:
                    pe.wait_ge(fT_ready, c)
                for y in range(G // 2):
                    mm = nc.tensor.transpose(bank(FB)[:, y * P:(y + 1) * P], fb[:, c % 2, 2 * y:2 * y + 2, :], ident[:])
                mm.then_inc(f_T, 1)

            def f_w(c):
                pe.wait_ge(fT_ready, c + 1)
                if c >= 1:
                    pe.wait_ge(g_ready, c)
                else:
                    pe.wait_ge(h_copied, len(IN_PSUM))
                for y in range(G):
                    mm = nc.tensor.matmul(ps[:, YG * BANK + y * P:YG * BANK + (y + 1) * P], fT[:, y // 2, :],
                                          wbd[:, y % 2, :], start=True, stop=True)
                mm.then_inc(y_done, 1)

            def b_sum(r, u, odd=0):
                for c in range(CB):
                    pe.wait_ge(b_l[c], r * BU + u + 1)
                    for s in range(2):
                        mm = nc.tensor.matmul(bank(BACC + odd), eg[:, u * CB + c, :, :], parts(u + odd, c)[:, s, :],
                                              start=(u == 0 and c == 0 and s == 0), stop=False,
                                              skip_group_check=True)
                    mm.then_inc(b_used, 1)

            def b_kept(r, odd=0):
                for c in range(CB):
                    for s in range(2):
                        rows = slice(r * BANK, (r + 1) * BANK) if isinstance(r, int) else bass.ds(r * BANK, BANK)
                        mm = nc.tensor.matmul(bank(BACC + odd), eg[:, RES * CB + c, :, :], kept[:, s, c, rows],
                                              start=False, stop=(c == CB - 1 and s == 1), skip_group_check=True)
                mm.then_inc(y_summed, 1)

            def b_finish(r):
                pe.wait_ge(y_copied, r + 1)
                if not (isinstance(r, int) and r == 0):
                    pe.wait_ge(y_scaled, r)
                for y in range(Y):
                    mm = nc.tensor.matmul(bank(BFIN)[:, y * D:(y + 1) * D], yT[:, y * P:(y + 1) * P], twoid[:],
                                          start=True, stop=True)
                mm.then_inc(y_turned, 1)

            for g in range(Y):
                sum_h(NB - 1, g)
            turn_h(0)
            turn_h(1)
            for s in range(NG + 2):
                b = b_units(s)
                if b[0]:
                    pe.wait_ge(g_ready, s - 1)
                for u in b[0]:
                    b_sum(0, u)
                for g in h_units(s):
                    sum_h(NB - 1, g)
                if 0 <= s - 1 < NG:
                    f_turn(s - 1)
                if 0 <= s - 1 < NG:
                    f_w(s - 1)
                if s + 2 < NG:
                    turn_h(s + 2)
                for u in b[1] + b[2] + b[3]:
                    b_sum(0, u)
            b_kept(0)

            def group_steps(r, odd):
                for u in range(BU):
                    b_sum(r, u, odd)
                    if u == 3:
                        b_finish(r - 1)
                b_kept(r, odd)

            row_groups(pe, group_steps)
            b_finish(NU - 1)

        @block.scalar
        def _(act):
            act.wait_ge(consts, 4)

            def h0_std(g):
                act.wait_ge(h0_var, g + 1)
                nc.scalar.activation(sd[:, g % 2, :], mv[:, g % 2, :, 1], ACT.Sqrt, bias=eps[:]).then_inc(h0_sd, 1)

            def h0T_copy(g):
                act.wait_ge(h0_T, g + 1)
                if g >= 1:
                    act.wait_ge(hw_done, g)
                nc.scalar.copy(fT[:], bank(2).rearrange("p (y r) -> p y r", r=P)).then_inc(h0T_ready, 1)

            def e_high(g):
                act.wait_ge(ef_ready, g + 1)
                nc.scalar.copy(eg[:, g * G:(g + 1) * G, 0, :], fb[:, g % 2, :, :]).then_inc(eh_ready, 1)

            def high(i, g):
                act.wait_ge(landed[g % NAT_SLOTS], landed_a(i, g))
                if not (isinstance(i, int) and i == 0 and g < 2):
                    act.wait_ge(t_summed, i * NU + g - 1)
                for y in range(Y):
                    a = (2 * g + y // 2) % 4
                    ins = nc.scalar.activation(ring[:, a, 0, (y % 2) * W:(y % 2 + 1) * W], nat[:, g % NAT_SLOTS, y * W:(y + 1) * W],
                                               ACT.Copy, accum_out=degp[:, g * Y + y, bass.ds(i, 1)])
                    if y % 2 == 1:
                        ins.then_inc(nat_h, 1)

            def keep_high(i, g):
                for c in range(0 if isinstance(i, int) and i == 0 else 1, CB):
                    wait_piece(act, i, g, c)
                    nc.scalar.copy(kept[:, 0, c, g * BANK:(g + 1) * BANK], piece(g, c)).then_inc(piece_h[c], 1)

            def copy_t(i):
                act.wait_ge(t_summed, (i + 1) * NU)
                if not (isinstance(i, int) and i == 0):
                    act.wait_ge(t_turned, i)
                nc.scalar.copy(tT[:], bank(TB, W)).then_inc(t_copied, 1)

            def t_split(i):
                act.wait_ge(t_turned, i + 1)
                nc.scalar.copy(th[:, :, 0, :], tiles(ACC, CB)).then_inc(t_high, 1)

            def block_steps(i, more=True):
                for g in range(NU):
                    if g == NU - 1:
                        copy_t(i)
                    if g < NU - 2:
                        high(i, g + 2)
                    elif more:
                        high(i + 1, g + 2 - NU)
                    if g == NU - 1:
                        t_split(i)
                    keep_high(i, g)

            nc.scalar.activation(first[:], eps[:], ACT.Sqrt)
            h0_std(0)
            h0_std(1)
            h0T_copy(0)
            high(0, 0)
            h0_std(2)
            high(0, 1)
            h0T_copy(1)
            e_high(0)
            e_high(1)
            h0_std(3)
            for k in range(NG):
                if k + 2 < NG:
                    h0T_copy(k + 2)
                for g in (2 * k, 2 * k + 1):
                    if g == NU - 1:
                        copy_t(0)
                    high(*((0, g + 2) if g < NU - 2 else (1, g + 2 - NU)))
                    if g == NU - 1:
                        t_split(0)
                    keep_high(0, g)
                    if g % 2 == 0 and 1 <= k < NG - 3:
                        h0_std(k + 3)
                if k + 2 < NG:
                    e_high(k + 2)
            with act.Fori(1, NB - 1) as i:
                block_steps(i)
            block_steps(NB - 1, more=False)

            def copy_h(g):
                act.wait_ge(h_summed, (NB - 1) * NU + g + 1)
                nc.scalar.copy(hT[:, g * BANK:(g + 1) * BANK], bank(IN_PSUM.index(g))).then_inc(h_copied, 1)

            def std(c, which, have, give):
                act.wait_ge(have, c + 1)
                nc.scalar.activation(sd[:, which, :], mv[:, which, :, 1], ACT.Sqrt, bias=eps[:]).then_inc(give, 1)

            def b_high(r, u, odd=0):
                act.wait_ge(landed[u % SLOTS], landed_b(r, u))
                if isinstance(r, int) and r == 0 and u < 2:
                    act.wait_ge(t_summed, NB * NU)
                for c in range(CB):
                    if not (isinstance(r, int) and r == 0 and u < 2):
                        act.wait_ge(b_used, (r * BU + u - 2) * CB + c + 1)
                    nc.scalar.copy(parts(u + odd, c)[:, 0, :], nat[:, u % SLOTS, c * BANK:(c + 1) * BANK]
                                   ).then_inc(b_h, 1)

            def make_f(c):
                act.wait_ge(x2_rs, c + 1)
                if c >= 2:
                    act.wait_ge(f_T, c - 1)
                for y in range(G):
                    a = nc.scalar.activation(fb[:, c % 2, y, :], xr[:, c * G + y, :], ACT.Relu,
                                             bias=nm[:, c % 2, y:y + 1], scale=rs[:, 2 + c % 2, y:y + 1])
                a.then_inc(f_ready, 1)

            for g in range(Y):
                if g in IN_PSUM:
                    copy_h(g)
            std(0, 0, hn_var, hn_sd)
            for s in range(NG + 2):
                b = b_units(s)
                for u in b[0]:
                    b_high(0, u)
                if 0 <= s - 1 < NG:
                    make_f(s - 1)
                for g in h_units(s):
                    if g in IN_PSUM:
                        copy_h(g)
                for u in b[1]:
                    b_high(0, u)
                if s + 1 < NG:
                    std(s + 1, (s + 1) % 2, hn_var, hn_sd)
                if 0 <= s - 1 < NG:
                    act.wait_ge(f_T, s)
                    if s > 1:
                        act.wait_ge(y_done, s - 1)
                    nc.scalar.copy(fT[:], bank(FB).rearrange("p (y r) -> p y r", r=P)).then_inc(fT_ready, 1)
                for u in b[2]:
                    b_high(0, u)
                if s < NG:
                    std(s, 2 + s % 2, x2_var, x2_sd)
                if 0 <= s - 1 < NG:
                    act.wait_ge(y_done, s)
                    nc.scalar.copy(eg[:, (s - 1) * G:s * G, 0, :], yg[:, :, 1, :]).then_inc(gh_ready, 1)
                for u in b[3]:
                    b_high(0, u)

            def copy_y(r, odd):
                act.wait_ge(y_summed, r + 1)
                if not (isinstance(r, int) and r == 0):
                    act.wait_ge(y_turned, r)
                nc.scalar.copy(yT[:], bank(BACC + odd)).then_inc(y_copied, 1)

            def store(r):
                act.wait_ge(final, r + 1)
                ks = slice(r * Y, (r + 1) * Y) if isinstance(r, int) else bass.ds(r * Y, Y)
                act.dma_start(out[:, ks, :], xr[:, ks, :]).then_inc(stored, 16)

            def group_steps(r, odd):
                for u in range(BU):
                    b_high(r, u, odd)
                    if u == 1:
                        copy_y(r - 1, 1 - odd)
                    if u == 12:
                        store(r - 1)

            row_groups(act, group_steps)
            copy_y(NU - 1, 1)
            store(NU - 1)
            act.wait_ge(stored, 16 * NU)

        @block.vector
        def _(dve):
            own = [0]

            def link(ins):
                own[0] += 1
                ins.then_inc(vec, 1)
                dve.wait_ge(vec, own[0])

            def moments(src, which, give):
                for y in range(G):
                    ins = nc.vector.bn_stats(st[:, which, y, :], src[:, y, :])
                link(ins)
                for y in range(G):
                    ins = nc.vector.bn_aggr(mv[:, which, y, :], st[:, which, y, :])
                ins.then_inc(give, 1)

            def reciprocal(which, have, c):
                dve.wait_ge(have, c + 1)
                link(nc.vector.reciprocal(rs[:, which, :], sd[:, which, :]))

            def h0_moments(g):
                dve.wait_ge(x_landed[g], 16)
                moments(xr[:, g * G:(g + 1) * G, :], g % 2, h0_var)

            def h0_normal(g):
                ks = slice(g * G, (g + 1) * G)
                mean, inv = (a.unsqueeze(2).to_broadcast([P, G, D]) for a in (mv[:, g % 2, :, 0], rs[:, g % 2, :]))
                reciprocal(g % 2, h0_sd, g)
                link(nc.vector.tensor_tensor(h0[:, ks, :], xr[:, ks, :], mean, ALU.subtract))
                nc.vector.scalar_tensor_tensor(out=h0[:, ks, :], in0=h0[:, ks, :], scalar=0.0, in1=inv,
                                               op0=ALU.max, op1=ALU.mult).then_inc(h0_ready, 1)

            def make_e(g):
                ks = slice(g * G, (g + 1) * G)
                dve.wait_ge(hw_done, g + 1)
                dve.wait_ge(h0_ready, g + 1)
                e = fb[:, g % 2, :, :]
                link(nc.vector.tensor_tensor(e, tiles(3), coef[:, ks].unsqueeze(2).to_broadcast([P, G, D]), ALU.mult))
                nc.vector.tensor_tensor(e, e, h0[:, ks, :], ALU.add).then_inc(ef_ready, 1)

            def e_low(g):
                ks = slice(g * G, (g + 1) * G)
                dve.wait_ge(ef_ready, g + 1)
                dve.wait_ge(eh_ready, g + 1)
                nc.vector.tensor_tensor(eg[:, ks, 1, :], fb[:, g % 2, :, :], eg[:, ks, 0, :].bitcast(F32), ALU.subtract
                                        ).then_inc(e_ready, 1)

            def residual(g):
                v = xr[:, g * G:(g + 1) * G, :]
                link(nc.vector.tensor_tensor(v, v, h0[:, g * G:(g + 1) * G, :], ALU.add))
                nc.vector.tensor_tensor(v, v, bet.unsqueeze(1).to_broadcast([P, G, D]), ALU.add).then_inc(xrb_ready, 1)

            def t_split(i):
                dve.wait_ge(t_high, i + 1)
                nc.vector.tensor_tensor(th[:, :, 1, :], tiles(ACC, CB), th[:, :, 0, :].bitcast(F32), ALU.subtract
                                        ).then_inc(t_ready, 1)

            def keep_low(i, g):
                to = slice(g * BANK, (g + 1) * BANK)
                for c in range(CB):
                    if c == 0 and not (isinstance(i, int) and i == 0):
                        wait_piece(dve, i, g, c)
                        nc.vector.tensor_copy(kept[:, 0, 0, to], piece(g, 0)).then_inc(piece_h[0], 1)
                    if g == NU - 1 and c == CB - 1:
                        t_split(i)
                    dve.wait_ge(piece_h[c], i * NU + g + 1)
                    nc.vector.tensor_tensor(kept[:, 1, c, to], piece(g, c), kept[:, 0, c, to].bitcast(F32),
                                            ALU.subtract).then_inc(piece_l, 1)

            def add_h(i, g):
                if g not in IN_SBUF:
                    return
                dve.wait_ge(h_summed, i * NU + g + 1)
                to = hT[:, g * BANK:(g + 1) * BANK]
                if isinstance(i, int) and i == 0:
                    nc.vector.tensor_copy(to, bank(ACC)).then_inc(h_added, 1)
                else:
                    nc.vector.tensor_tensor(to, bank(ACC), to, ALU.add).then_inc(h_added, 1)

            def block_steps(i):
                for g in range(NU):
                    add_h(i - 1, g)
                    keep_low(i, g)

            h0_moments(0)
            h0_normal(0)
            h0_moments(1)
            dve.wait_ge(small_landed, 16)
            link(nc.vector.tensor_tensor(parp[:], par[:, :, 0], par[:, :, 1], ALU.mult))
            nc.vector.tensor_scalar(coef[:, 0:UT], sm[:, DIAG:DIAG + UT], parp[:, 0:1], None, ALU.mult)
            link(nc.vector.tensor_scalar(coef[:, UT:NT], sm[:, DIAG + UT:DIAG + NT], parp[:, 1:2], None, ALU.mult))
            h0_normal(1)
            h0_moments(2)
            make_e(0)
            e_low(0)
            h0_normal(2)
            make_e(1)
            h0_moments(3)
            e_low(1)
            for k in range(NG):
                keep_low(0, 2 * k)
                if k + 3 < NG:
                    h0_normal(k + 3)
                if k + 2 < NG:
                    make_e(k + 2)
                keep_low(0, 2 * k + 1)
                if k + 2 < NG:
                    e_low(k + 2)
                if k + 4 < NG:
                    h0_moments(k + 4)
                for g in ([], [], [0], [1, 2], [3, 4])[k]:
                    residual(g)
            dve.wait_ge(xrb_ready, NG)
            block_steps(1)
            with dve.Fori(2, NB) as i:
                block_steps(i)

            def b_low(r, u, odd=0):
                for c in range(1 if isinstance(r, int) and r == 0 else CB):
                    dve.wait_ge(b_h, (r * BU + u) * CB + c + 1)
                    nc.vector.tensor_tensor(parts(u + odd, c)[:, 1, :], nat[:, u % SLOTS, c * BANK:(c + 1) * BANK],
                                            parts(u + odd, c)[:, 0, :].bitcast(F32), ALU.subtract).then_inc(b_l[c], 1)

            def x2_factors(c):
                reciprocal(2 + c % 2, x2_sd, c)
                if c >= 2:
                    dve.wait_ge(f_ready, c - 1)
                nc.vector.scalar_tensor_tensor(out=nm[:, c % 2, :], in0=mv[:, 2 + c % 2, :, 0], scalar=-1.0,
                                               in1=rs[:, 2 + c % 2, :], op0=ALU.mult, op1=ALU.mult).then_inc(x2_rs, 1)

            dve.wait_ge(nat_h, NB * NU * 2)
            link(nc.vector.tensor_reduce(rdeg[:, 0, :], degp[:], AX.X, ALU.add))
            link(nc.vector.tensor_scalar(rdeg[:, 1, :], rdeg[:, 0, :], 1.0, None, ALU.add))
            link(nc.vector.reciprocal(rdeg[:, 2, :], rdeg[:, 1, :]))

            for g in range(Y):
                add_h(NB - 1, g)
            def h_moments(c):
                dve.wait_ge(h_turned, c + 1)
                moments(tiles(HB + c % 2), c % 2, hn_var)

            h_moments(0)
            for s in range(NG + 2):
                b = b_units(s)
                if s < NG:
                    reciprocal(s % 2, hn_sd, s)
                    nc.vector.tensor_tensor(hn[:, s], tiles(HB + s % 2),
                                            mv[:, s % 2, :, 0].unsqueeze(2).to_broadcast([P, G, D]),
                                            ALU.subtract).then_inc(h_centred, 1)
                for u in b[0]:
                    b_low(0, u)
                for g in h_units(s):
                    add_h(NB - 1, g)
                if s + 1 < NG:
                    h_moments(s + 1)
                for u in b[1]:
                    b_low(0, u)
                if s < NG:
                    dve.wait_ge(x2_ready, s + 1)
                    moments(xr[:, s * G:(s + 1) * G, :], 2 + s % 2, x2_var)
                for u in b[2]:
                    b_low(0, u)
                if s < NG:
                    x2_factors(s)
                if 0 <= s - 1 < NG:
                    dve.wait_ge(gh_ready, s)
                    ks = slice((s - 1) * G, s * G)
                    nc.vector.tensor_tensor(eg[:, ks, 1, :], yg[:, :, 1, :], eg[:, ks, 0, :].bitcast(F32), ALU.subtract)
                    nc.vector.tensor_tensor(xr[:, ks, :], yg[:, :, 0, :], xr[:, ks, :], ALU.add).then_inc(g_ready, 1)
                for u in b[3]:
                    b_low(0, u)
            dve.wait_ge(b_l[1], BU)

            def finish(r):
                dve.wait_ge(y_turned, r + 1)
                ks = slice(r * Y, (r + 1) * Y) if isinstance(r, int) else bass.ds(r * Y, Y)
                if not (isinstance(r, int) and r == 0):
                    dve.wait_ge(final, r)
                v = fb[:, 0, 0:Y, :]
                nc.vector.tensor_tensor(v, tiles(BFIN, Y), rdeg[:, 2, ks].unsqueeze(2).to_broadcast([P, Y, D]),
                                        ALU.mult).then_inc(y_scaled, 1)
                dve.wait_ge(y_scaled, r + 1)
                nc.vector.tensor_tensor(xr[:, ks, :], v, xr[:, ks, :], ALU.add).then_inc(final, 1)

            def group_steps(r, odd):
                for u in range(BU):
                    b_low(r, u, odd)
                    if u == 8:
                        finish(r - 1)

            row_groups(dve, group_steps)
            finish(NU - 1)


def laid_out(x, adj, L0_gnn_W_u, L0_gnn_diag_u, L0_gnn_par_u, L0_gnn_W_i, L0_gnn_diag_i, L0_gnn_par_i,
             L0_gnn_ln_gamma, L0_gnn_ln_beta, L1_gnn_W):
    import numpy as np

    adj = np.asarray(adj)
    small = np.zeros((P, SMALL), np.asarray(x).dtype)
    for n, w in enumerate((L0_gnn_W_u, L0_gnn_W_i)):
        small[0:D, WUI + 2 * n * D:WUI + (2 * n + 1) * D] = w
        small[D:P, WUI + (2 * n + 1) * D:WUI + (2 * n + 2) * D] = w
    for m in range(2):
        wt = np.asarray(L1_gnn_W)[:, m * D:(m + 1) * D].T
        small[0:D, WBD + m * D:WBD + (m + 1) * D] = wt
        small[D:P, WBD + (2 + m) * D:WBD + (3 + m) * D] = wt
    small[:, DIAG:PAR] = np.concatenate([L0_gnn_diag_u, L0_gnn_diag_i]).reshape(NT, P).T
    small[:, PAR:PAR + 2] = L0_gnn_par_u
    small[:, PAR + 2:GAM] = L0_gnn_par_i
    small[:, GAM:BET] = L0_gnn_ln_gamma
    small[:, BET:SMALL] = L0_gnn_ln_beta
    return {
        "x": np.ascontiguousarray(np.asarray(x).reshape(NT, P, D).transpose(1, 0, 2)),
        "units": np.ascontiguousarray(adj.reshape(NU, Y, P, NB, W).transpose(3, 0, 2, 1, 4)).reshape(NB * NU * P, Y * W),
        "units_T": np.ascontiguousarray(
            adj.reshape(NU, BANK, NB, CB, P).transpose(0, 2, 4, 3, 1)).reshape(NU * NB * P, CB * BANK),
        "small": small,
    }


def kernel(**inputs):
    import numpy as _np
    import concourse.bacc as _bacc
    from concourse import mybir as _mybir
    from concourse.bass_utils import run_bass_kernel_spmd as _run

    nc = _bacc.Bacc("TRN2", target_bir_lowering=False, num_devices=1)
    arrays, args = {}, []
    for name, a in laid_out(**inputs).items():
        arrays[f"in_{name}"] = a
        args.append(nc.dram_tensor(f"in_{name}", a.shape, _mybir.dt.from_np(a.dtype), kind="ExternalInput").ap())
    args.append(nc.dram_tensor("out", (P, NT, D), _mybir.dt.float32, kind="ExternalOutput").ap())
    build(nc, *args)
    r = _run(nc, [arrays], core_ids=[0])
    out = _np.asarray(r.results[0]["out"])
    return _np.ascontiguousarray(out.transpose(1, 0, 2)).reshape(N, D)
```
